# Optimizing a Trainium2 kernel written in Bass

```python
import numpy as np
import jax
import jax.numpy as jnp

def _softmax(x, axis=-1):
    return jax.nn.softmax(x, axis=axis)

def _gelu(x):
    return jax.nn.gelu(x, approximate=True)

def _silu(x):
    return jax.nn.silu(x)

def _sigmoid(x):
    return jax.nn.sigmoid(x)

def _layernorm(x, axis=-1, eps=1e-05):
    m = jnp.mean(x, axis=axis, keepdims=True)
    v = jnp.var(x, axis=axis, keepdims=True)
    return (x - m) / jnp.sqrt(v + eps)

def _scatter_add(tgt, idx, src, axis=0):
    return tgt.at[idx].add(src)

def _segment_sum(src, seg, n):
    return jax.ops.segment_sum(src, seg, n)
kernel_name = 'mk_adj_resnorm_d4_adj_r2_6f4469'

def setup_inputs(seed: int=0):
    np.random.seed(seed)
    _w = jnp.asarray

    def _rec_inputs():
        import jax
        import jax.numpy as jnp
        _gk = jax.random.key(seed)
        x = -0.0005146 + 1 * jax.random.normal(jax.random.fold_in(_gk, 1), (8, 1024, 128), jnp.float32)
        _a = jax.random.bernoulli(jax.random.fold_in(_gk, 2), 0.015625, (8, 1024, 1024))
        adj = _a.astype(jnp.int32)
        return (x, adj)
    x, adj = _rec_inputs()

    def _L0_gnn_setup():
        import jax, jax.numpy as jnp
        import numpy as np
        B, N, C, OUT, S = (4, 1024, 128, 128, 25)
        DENSITY = 0.008
        key = jax.random.key(seed)
        kA, kX, kW = jax.random.split(key, 3)
        A = jax.random.bernoulli(kA, DENSITY, (B, N, N)).astype(jnp.int32)
        X = jax.random.normal(kX, (B, N, C), dtype=jnp.float32)
        W = jax.random.normal(kW, (2 * C, OUT), dtype=jnp.float32) * np.float32(1.0 / np.sqrt(2 * C))
        b = jnp.zeros((OUT,), dtype=jnp.float32)
        return {'A': A, 'X': X, 'W': W, 'b': b}
    _L0_gnn_all = _L0_gnn_setup()
    _L0_gnn_in = {k: v for k, v in _L0_gnn_all.items() if k in ('W', 'b')}
    del _L0_gnn_all

    def _L1_gnn_setup():
        import jax, jax.numpy as jnp
        import numpy as np
        ALPHA = 0.2
        SCALE_ATT = 1.0
        NEG_MASK = -9000000000000000.0
        key = jax.random.key(seed)
        k1, k2, k3, k4 = jax.random.split(key, 4)
        B, N, Din, Dout = (32, 512, 128, 128)
        h = jax.random.normal(k1, (B, N, Din), dtype=jnp.float32)
        adj = jax.random.randint(k2, (B, N, N), 0, 2, dtype=jnp.int32)
        W = jax.random.normal(k3, (Dout, Din), dtype=jnp.float32) * (1.0 / np.sqrt(Din))
        b = jnp.zeros((Dout,), dtype=jnp.float32)
        a = jax.random.normal(k4, (2 * Dout,), dtype=jnp.float32) * 0.1
        return {'h': h, 'adj': adj, 'W': W, 'b': b, 'a': a}
    _L1_gnn_all = _L1_gnn_setup()
    _L1_gnn_in = {k: v for k, v in _L1_gnn_all.items() if k in ('W', 'b', 'a')}
    del _L1_gnn_all

    def _L2_gnn_setup():
        import jax, jax.numpy as jnp
        import numpy as np
        ALPHA = 0.2
        NEG_BIG = -9000000000000000.0
        key = jax.random.key(seed)
        k1, k2, k3, k4 = jax.random.split(key, 4)
        B, N, Fin, Fout = (16, 512, 128, 128)
        h = jax.random.normal(k1, (B, N, Fin), dtype=jnp.float32)
        adj = jax.random.randint(k2, (B, N, N), 0, 2, dtype=jnp.int32)

        def xavier(k, shape, gain=1.414):
            fan_in, fan_out = (shape[0], shape[1])
            bound = gain * np.sqrt(6.0 / (fan_in + fan_out))
            return jax.random.uniform(k, shape, jnp.float32, -bound, bound)
        W = xavier(k3, (Fin, Fout))
        a = xavier(k4, (2 * Fout, 1))
        return {'h': h, 'adj': adj, 'W': W, 'a': a}
    _L2_gnn_all = _L2_gnn_setup()
    _L2_gnn_in = {k: v for k, v in _L2_gnn_all.items() if k in ('W', 'a')}
    del _L2_gnn_all

    def _L3_gnn_setup():
        import jax, jax.numpy as jnp
        import numpy as np
        B, N, H = (64, 512, 128)
        NEG = -1000.0
        key = jax.random.key(seed)
        k = jax.random.split(key, 6)
        s = 1.0 / np.sqrt(H).astype(np.float32)
        return {'inputs': jax.random.normal(k[0], (B, N, H), dtype=jnp.float32), 'dep_adjs': jax.random.randint(k[1], (B, N, N), 0, 2, dtype=jnp.int32), 'att_W': jax.random.normal(k[2], (H, H), dtype=jnp.float32) * s, 'W0': jax.random.normal(k[3], (H, H), dtype=jnp.float32) * s, 'b0': jnp.zeros((H,), dtype=jnp.float32), 'W1': jax.random.normal(k[4], (H, H), dtype=jnp.float32) * s, 'b1': jnp.zeros((H,), dtype=jnp.float32)}
    _L3_gnn_all = _L3_gnn_setup()
    _L3_gnn_in = {k: v for k, v in _L3_gnn_all.items() if k in ('att_W', 'W0', 'b0', 'W1', 'b1')}
    del _L3_gnn_all
    return {'x': x, 'adj': adj, 'L0_gnn_W': _L0_gnn_in['W'], 'L0_gnn_b': _L0_gnn_in['b'], 'L1_gnn_W': _L1_gnn_in['W'], 'L1_gnn_b': _L1_gnn_in['b'], 'L1_gnn_a': _L1_gnn_in['a'], 'L2_gnn_W': _L2_gnn_in['W'], 'L2_gnn_a': _L2_gnn_in['a'], 'L3_gnn_att_W': _L3_gnn_in['att_W'], 'L3_gnn_W0': _L3_gnn_in['W0'], 'L3_gnn_b0': _L3_gnn_in['b0'], 'L3_gnn_W1': _L3_gnn_in['W1'], 'L3_gnn_b1': _L3_gnn_in['b1']}

def reference(x, adj, L0_gnn_W, L0_gnn_b, L1_gnn_W, L1_gnn_b, L1_gnn_a, L2_gnn_W, L2_gnn_a, L3_gnn_att_W, L3_gnn_W0, L3_gnn_b0, L3_gnn_W1, L3_gnn_b1):
    import jax
    import jax.numpy as jnp

    def _L0_gnn_ref(A, X, W, b):
        import jax, jax.numpy as jnp
        import numpy as np
        B, N, C, OUT, S = (4, 1024, 128, 128, 25)
        DENSITY = 0.008
        mask = A != 0
        neg_inf = jnp.float32(-jnp.inf)
        pri = -jnp.arange(N, dtype=jnp.float32)
        scores = jnp.where(mask, pri, neg_inf)
        vals, idx = jax.lax.top_k(scores, S)
        valid = vals > neg_inf
        feats = jax.vmap(lambda x, i: x[i])(X, idx)
        feats = jnp.where(valid[..., None], feats, neg_inf)
        agg = feats.max(axis=2)
        degree = mask.sum(axis=-1)
        agg = jnp.where((degree <= S)[..., None], jnp.maximum(agg, 0.0), agg)
        h = jnp.concatenate([X, agg], axis=-1)
        out = jax.nn.relu(jnp.einsum('bnf,fo->bno', h, W) + b)
        return out

    def _L1_gnn_ref(h, adj, W, b, a):
        import jax, jax.numpy as jnp
        import numpy as np
        ALPHA = 0.2
        SCALE_ATT = 1.0
        NEG_MASK = -9000000000000000.0
        z = jnp.einsum('bnd,od->bno', h, W) + b
        Dout = z.shape[-1]
        a1, a2 = (a[:Dout], a[Dout:])
        s1 = jnp.einsum('bnd,d->bn', z, a1)
        s2 = jnp.einsum('bnd,d->bn', z, a2)
        e = jax.nn.leaky_relu(s1[:, :, None] + s2[:, None, :], negative_slope=ALPHA)
        e = jnp.where(adj > 0, e, NEG_MASK) * SCALE_ATT
        attention = jax.nn.softmax(e, axis=-1)
        h_prime = jnp.einsum('bij,bjd->bid', attention, z)
        return jax.nn.elu(h_prime)

    def _L2_gnn_ref(h, adj, W, a):
        import jax, jax.numpy as jnp
        import numpy as np
        ALPHA = 0.2
        NEG_BIG = -9000000000000000.0
        Fout = W.shape[1]
        Wh = jnp.einsum('bnf,fo->bno', h, W)
        a1, a2 = (a[:Fout, 0], a[Fout:, 0])
        f1 = Wh @ a1
        f2 = Wh @ a2
        e = jax.nn.leaky_relu(f1[:, :, None] + f2[:, None, :], negative_slope=ALPHA)
        attention = jnp.where(adj > 0, e, jnp.float32(NEG_BIG))
        attention = jax.nn.softmax(attention, axis=2)
        h_prime = jnp.einsum('bij,bjo->bio', attention, Wh)
        return jax.nn.elu(h_prime)

    def _L3_gnn_ref(inputs, dep_adjs, att_W, W0, b0, W1, b1):
        import jax, jax.numpy as jnp
        import numpy as np
        B, N, H = (64, 512, 128)
        NEG = -1000.0
        mask = jnp.where(dep_adjs == 1, 0.0, NEG).astype(inputs.dtype)
        q = jnp.einsum('bnh,hk->bnk', inputs, att_W)
        score = jnp.einsum('bnk,bmk->bnm', q, inputs) / jnp.sqrt(jnp.asarray(H, inputs.dtype))
        att_adjs = jax.nn.softmax(score + mask, axis=-1)
        x = inputs
        for W, b in ((W0, b0), (W1, b1)):
            xw = jnp.einsum('bnh,hk->bnk', x, W) + b
            x = jnp.tanh(jnp.einsum('bnm,bmk->bnk', att_adjs, xw))
        return x
    x = _layernorm(x + _L0_gnn_ref(adj, x, L0_gnn_W, L0_gnn_b), axis=-1)
    x = _layernorm(x + _L1_gnn_ref(x, adj, L1_gnn_W, L1_gnn_b, L1_gnn_a), axis=-1)
    x = _layernorm(x + _L2_gnn_ref(x, adj, L2_gnn_W, L2_gnn_a), axis=-1)
    x = _layernorm(x + _L3_gnn_ref(x, adj, L3_gnn_att_W, L3_gnn_W0, L3_gnn_b0, L3_gnn_W1, L3_gnn_b1), axis=-1)
    return x

_drawn_inputs = setup_inputs


def setup_inputs(seed=0):
    import zlib

    import numpy as np

    out = dict(_drawn_inputs(seed))
    spreads = {'L0_gnn_b': (0.0, 0.1),
     'L1_gnn_b': (0.0, 0.1),
     'L3_gnn_b0': (0.0, 0.1),
     'L3_gnn_b1': (0.0, 0.1)}
    factors = {}
    for name, (base, spread) in spreads.items():
        noise = np.random.default_rng([zlib.crc32(name.encode()), seed]).standard_normal(out[name].shape)
        drawn = base * np.exp(spread * noise) if base else spread * noise
        out[name] = jnp.asarray(drawn.astype(out[name].dtype))
    for name, factor in factors.items():
        out[name] = (out[name] * factor).astype(out[name].dtype)
    return out
```

```python
import concourse.bass as bass
from concourse import mybir
from contextlib import ExitStack

F32 = mybir.dt.float32
BF16 = mybir.dt.bfloat16
I32 = mybir.dt.int32
U32 = mybir.dt.uint32
U8 = mybir.dt.uint8
ALU = mybir.AluOpType
ACT = mybir.ActivationFunctionType
AX = mybir.AxisListType

P = 128
SAMPLES = 25
NEG_SLOPE = 0.2
EPS = 1e-5
GROUP = 4
TOP = 32
RING = 4
LOWEST = -3.0e38
RSQRT_GUESS = float(0x5f3759df)


class Signal:

    def __init__(self, ctx, nc, name, per, unit=1, ahead=0):
        self.sem = ctx.enter_context(nc.semaphore(name))
        self.per, self.unit, self.ahead = per, unit, ahead

    def at(self, b, k):
        return b * (self.per * self.unit) + (k + self.ahead) * self.unit

    def raised_by(self, instruction):
        return instruction.then_inc(self.sem, self.unit)


class Steps:

    def __init__(self, eng):
        self.settle = eng.drain

    def done(self, instruction):
        pass

    def link(self, instruction):
        self.settle()


FEED = {1: [(1, 1)], 3: [(1, 2)], 5: [(1, 3)], 8: [(2, 0)]}
SIDE = {2: [("search", 1, 1), ("pool", 1, 0)],
        4: [("search", 1, 2), ("pool", 1, 1)],
        5: [("pool", 1, 2)],
        6: [("search", 1, 3), ("pool", 1, 3)],
        7: [("pool", 1, 4)],
        8: [("pool", 1, 5), ("search", 2, 0), ("pool", 1, 6), ("pool", 1, 7)]}


def exists(b, ahead, graphs, in_loop):
    return in_loop or b + ahead < graphs


def build_graph_layers(nc, x, adj, w0, b0, w1, b1, a1, w2, a2, watt, w3a, b3a, w3b, b3b, out):
    B, N, C = x.shape
    T = N // P
    PAIRS = T // 2
    G = N // GROUP
    GP = P // GROUP
    LOOPED = B - 2
    assert C == P and T % RING == 0 and LOOPED % 2 == 0

    x_rows = x.rearrange("b n c -> (b n) c")
    x_tiles = x.rearrange("b (t p) c -> b p t c", p=P)
    out_tiles = out.rearrange("b (t p) c -> b p t c", p=P)
    adj_tiles = adj.rearrange("b (t p) m -> b t p m", p=P)

    with ExitStack() as ctx:
        def sb(name, shape, dt=F32):
            return ctx.enter_context(nc.sbuf_tensor(name, shape, dt))

        def ps(name, shape, dt=F32):
            return ctx.enter_context(nc.psum_tensor(name, shape, dt))

        def signal(name, per, unit=1, ahead=0):
            return Signal(ctx, nc, name, per, unit, ahead)

        ident = sb("ident", [P, P])
        ident_bf = sb("ident_bf", [P, P], BF16)
        ones = sb("ones", [P, P])
        pack_w = sb("pack_w", [P, GP], BF16)
        group_key = sb("group_key", [P, G])
        w0_sb = sb("w0_sb", [P, 2, P])
        b0_row = sb("b0_row", [1, P])
        gat_w = [sb(f"gat_w{l}", [P, P]) for l in range(2)]
        gat_wt = [sb(f"gat_wt{l}", [P, P]) for l in range(2)]
        gat_a = [sb(f"gat_a{l}", [P, 2]) for l in range(2)]
        gat_srow = [sb(f"gat_srow{l}", [P, 2, P]) for l in range(2)]
        b1_row = sb("b1_row", [1, P])
        b1_col = sb("b1_col", [P, 1])
        score_bias = sb("score_bias", [P, 2])
        neg_score_bias = sb("neg_score_bias", [P, 2])
        watt_sb = sb("watt_sb", [P, P])
        w3_sb = [sb(f"w3_sb{l}", [P, P]) for l in range(2)]
        b3_row = [sb(f"b3_row{l}", [1, P]) for l in range(2)]

        adj_in = sb("adj_in", [P, 2, N], I32)
        adj_bf = sb("adj_bf", [P, 2, N], BF16)
        adj_u8 = [sb(f"adj_u8{i}", [P, T, N], U8) for i in range(2)]
        adj_t = [sb(f"adj_t{i}", [P, T, N], BF16) for i in range(2)]
        degree = [sb(f"degree{i}", [P, T]) for i in range(2)]
        isolated = [sb(f"isolated{i}", [P, T]) for i in range(2)]
        connected = [sb(f"connected{i}", [P, T]) for i in range(2)]
        pool_floor = [sb(f"pool_floor{i}", [P, T]) for i in range(2)]
        keys = sb("keys", [P, 2, G])
        top_keys = sb("top_keys", [P, 2, TOP])
        top_int = sb("top_int", [P, 2, TOP], I32)
        top_base = sb("top_base", [P, 2, TOP], I32)
        top_bit = sb("top_bit", [P, GROUP, 2, TOP], I32)
        members = sb("members", [P, 2, GROUP, TOP])
        top_members = sb("top_members", [P, 2, TOP])
        missing = sb("missing", [P, 2, SAMPLES])
        row_base = sb("row_base", [P, 1])
        row_f = sb("row_f", [P, 2, SAMPLES])
        rows = sb("rows", [P, T, SAMPLES], U32)
        gathered = sb("gathered", [P, RING, SAMPLES * C])
        pooled = sb("pooled", [P, T, C])
        xs = [sb(f"xs{i}", [P, T, C]) for i in range(2)]
        xt = sb("xt", [P, N])
        below = sb("below", [P, N])
        above = sb("above", [P, N])
        work = sb("work", [P, 2, N])
        probs_t = sb("probs_t", [P, T, N])
        pooled_t = probs_t[:, 0, :]
        gat_arep = [work[:, 0, l * 2 * P:(l + 1) * 2 * P].rearrange("p (h c) -> p h c", h=2) for l in range(2)]
        b1_rep = work[:, 1, 0:P]
        group_key_i = below[:, 0:G].bitcast(I32)
        values = sb("values", [P, T, C + 1])
        head = xt[:, :].rearrange("p (t c) -> p t c", t=T)
        zsel = sb("zsel", [T, T, P])
        value_sum = sb("value_sum", [T, C + 1])
        top_score = sb("top_score", [P, 1])
        neg_top = sb("neg_top", [P, 1])
        shift = sb("shift", [P, 2])
        col_score = sb("col_score", [P, T])
        col_gap = sb("col_gap", [P, T])
        col_gap8 = sb("col_gap8", [P, T])
        recip = sb("recip", [P, T])
        neg_max = sb("neg_max", [P, T])
        row_sum = sb("row_sum", [P, T])
        stats = sb("stats", [P, T, 6])
        moments = sb("moments", [P, T, 2])
        rstd = sb("rstd", [P, T])
        spread = sb("spread", [P, T])
        guess = sb("guess", [P, T], I32)
        error = sb("error", [P, T])

        turn = ps("turn", [P, T, P], BF16)
        packed = ps("packed", [P, 2, G])
        big = ps("big", [P, 4 * 512])
        side = ps("side", [P, N])
        low, high = big[:, 0:N], big[:, N:2 * N]
        low_t = low.rearrange("p (t c) -> p t c", t=T)
        high_t = high.rearrange("p (t c) -> p t c", t=T)
        heads = big[:, :].rearrange("p (t c) -> p t c", t=T)
        side_t = side[:, :].rearrange("p (t c) -> p t c", t=T)
        halves = [slice(0, 512), slice(512, 1024)]

        weights = ctx.enter_context(nc.semaphore("weights"))
        consts = ctx.enter_context(nc.semaphore("consts"))
        reps_ready = ctx.enter_context(nc.semaphore("reps_ready"))
        setup_psum = ctx.enter_context(nc.semaphore("setup_psum"))
        setup_done = ctx.enter_context(nc.semaphore("setup_done"))
        adj_loaded = [signal(f"adj_loaded{i}", T // 2, 16) for i in range(2)]
        x_loaded = [signal(f"x_loaded{i}", 1, 8) for i in range(2)]
        out_stored = signal("out_stored", 1, 16, ahead=1)
        adj_converted = signal("adj_converted", T)
        adj_narrowed = signal("adj_narrowed", T)
        adj_turned = signal("adj_turned", T)
        adj_t_ready = signal("adj_t_ready", T)
        packed_ready = signal("packed_ready", PAIRS)
        packed_read = signal("packed_read", PAIRS)
        rows_ready = signal("rows_ready", PAIRS)
        rows_gathered = [signal(f"rows_gathered{i}", T // RING * SAMPLES, 16) for i in range(RING)]
        gathers_begun = ctx.enter_context(nc.semaphore("gathers_begun"))
        rows_pooled = signal("rows_pooled", T)
        pooled_turned = signal("pooled_turned", 1)
        pooled_t_ready = signal("pooled_t_ready", 1)
        x_turned = signal("x_turned", 4)
        xt_ready = signal("xt_ready", 4)
        sage_psum = signal("sage_psum", 1)
        iso_turned = signal("iso_turned", 1)
        zsel_ready = signal("zsel_ready", 1)
        x_normed = signal("x_normed", 4, ahead=1)
        scores_psum = signal("scores_psum", 2)
        shifts_ready = signal("shifts_ready", 2)
        bends_ready = signal("bends_ready", 2)
        z_psum = signal("z_psum", 2)
        z_ready = signal("z_ready", 2)
        sum_psum = signal("sum_psum", 2)
        sum_ready = signal("sum_ready", 2)
        gat_logit = signal("gat_logit", 2 * T)
        gat_exp = signal("gat_exp", 2 * T)
        gat_probs = signal("gat_probs", 2 * T)
        gat_heads = signal("gat_heads", 2)
        elu_in = signal("elu_in", 2)
        elu_exp = signal("elu_exp", 2)
        q_psum = signal("q_psum", 1)
        q_ready = signal("q_ready", 1)
        xw_psum = signal("xw_psum", 2)
        xw_ready = signal("xw_ready", 2)
        logits_psum = signal("logits_psum", T)
        row_max = signal("row_max", T)
        att_exp = signal("att_exp", T)
        att_masked = signal("att_masked", T)
        att_turned = signal("att_turned", T)
        att_t_ready = signal("att_t_ready", T)
        recip_ready = signal("recip_ready", 1)
        att_heads = signal("att_heads", 4)
        att_tanh = signal("att_tanh", 2 * T, ahead=1)
        y_turned = signal("y_turned", 1)
        y_ready = signal("y_ready", 1)

        block = ctx.enter_context(nc.Block())
        N_CONST = 6 + GROUP
        loads = [(w0_sb[:, :, :], w0.rearrange("(h p) o -> p h o", p=P)),
                 (b0_row[:, :], b0.rearrange("(a c) -> a c", a=1)),
                 (gat_w[0][:, :], w1), (gat_w[1][:, :], w2),
                 (gat_a[0][:, :], a1.rearrange("(h p) -> p h", p=P)),
                 (gat_a[1][:, :], a2.rearrange("(h p) a -> p (h a)", p=P)),
                 (b1_row[:, :], b1.rearrange("(a c) -> a c", a=1)),
                 (b1_col[:, :], b1.rearrange("(p a) -> p a", a=1)),
                 (watt_sb[:, :], watt), (w3_sb[0][:, :], w3a), (w3_sb[1][:, :], w3b),
                 (b3_row[0][:, :], b3a.rearrange("(a c) -> a c", a=1)),
                 (b3_row[1][:, :], b3b.rearrange("(a c) -> a c", a=1))]
        WEIGHTS_IN = 16 * len(loads)

        @block.sync
        def _(sp):
            def load_adj(b, t):
                if not (isinstance(b, int) and b == 0 and t < 2):
                    sp.wait_ge(adj_narrowed.sem, adj_narrowed.at(b, t - 1))
                adj_loaded[t % 2].raised_by(sp.dma_start(adj_in[:, t % 2, :], adj_tiles[b, t]))

            def load_x(b, slot):
                if not (isinstance(b, int) and b < 2):
                    sp.wait_ge(out_stored.sem, out_stored.at(b - 1, 0))
                sp.dma_start(xs[slot][:, :, :], x_tiles[b]).then_inc(x_loaded[slot].sem, 16)

            def graph(b, slot, in_loop):
                if exists(b, 1, B, in_loop):
                    load_x(b + 1, 1 - slot)
                    for t in range(2, T):
                        load_adj(b + 1, t)
                if exists(b, 2, B, in_loop):
                    for t in range(2):
                        load_adj(b + 2, t)
                sp.wait_ge(x_normed.sem, x_normed.at(b, 4))
                out_stored.raised_by(sp.dma_start(out_tiles[b], xs[slot][:, :, :]))

            sp.sem_inc(out_stored.sem, out_stored.unit)
            for t in range(2):
                load_adj(0, t)
            for dst, src in loads:
                with nc.allow_non_contiguous_dma(reason="small weights"):
                    sp.dma_start(dst, src).then_inc(weights, 16)
            for t in range(2, T):
                load_adj(0, t)
            for t in range(2):
                load_adj(1, t)
            load_x(0, 0)
            with sp.Fori(0, LOOPED // 2) as two:
                graph(two * 2, 0, True)
                graph(two * 2 + 1, 1, True)
            for b in range(LOOPED, B):
                graph(b, b % 2, False)
            sp.wait_ge(out_stored.sem, out_stored.at(B, 0))

        @block.gpsimd
        def _(pool):
            nc.gpsimd.memset(ident[:, :], 0.0).then_inc(consts, 1)
            nc.gpsimd.memset(pack_w[:, :], 0.0).then_inc(consts, 1)
            nc.gpsimd.memset(ones[:, :], 1.0).then_inc(consts, 1)
            nc.gpsimd.iota(group_key_i, pattern=[[-(1 << GROUP), G]], base=G << GROUP,
                           channel_multiplier=0).then_inc(consts, 1)
            pool.wait_ge(consts, 4)
            nc.gpsimd.affine_select(out=ident[:, :], in_=ident[:, :], compare_op=ALU.not_equal, fill=1.0,
                                    base=0, pattern=[[-1, P]], channel_multiplier=1).then_inc(consts, 1)
            for bit in range(GROUP):
                nc.gpsimd.affine_select(out=pack_w[:, :], in_=pack_w[:, :], compare_op=ALU.not_equal,
                                        fill=float(1 << bit), base=bit, pattern=[[GROUP, GP]],
                                        channel_multiplier=-1).then_inc(consts, 1)
                pool.wait_ge(consts, 6 + bit)
            nc.gpsimd.memset(values[:, :, C:C + 1], 1.0).then_inc(consts, 1)

            def gather(b, t):
                if t % 2 == 0:
                    pool.wait_ge(rows_ready.sem, rows_ready.at(b, t // 2 + 1))
                if not (isinstance(b, int) and b == 0 and t < RING):
                    pool.wait_ge(rows_pooled.sem, rows_pooled.at(b, t - RING + 1))
                pool.sem_inc(gathers_begun, 1)
                for k in range(SAMPLES):
                    rows_gathered[t % RING].raised_by(pool.indirect_dma_start(
                        out=gathered[:, t % RING, k * C:(k + 1) * C], out_offset=None, in_=x_rows,
                        in_offset=bass.IndirectOffsetOnAxis(ap=rows[:, t, k:k + 1], axis=0),
                        bounds_check=B * N - 1, oob_is_err=False))

            for t in range(T):
                gather(0, t)
            with pool.Fori(1, B) as b:
                for t in range(T):
                    gather(b, t)

        @block.scalar
        def _(act):
            def feed(b, slot, pair, reused):
                if pair == 0 and reused:
                    act.wait_ge(att_masked.sem, att_masked.at(b - 2, T))
                for t in (2 * pair, 2 * pair + 1):
                    act.wait_ge(adj_loaded[t % 2].sem, adj_loaded[t % 2].at(b, t // 2 + 1))
                    adj_converted.raised_by(nc.scalar.activation(
                        adj_bf[:, t % 2, :], adj_in[:, t % 2, :], ACT.Copy,
                        accum_out=degree[slot][:, t:t + 1]))
                    adj_narrowed.raised_by(nc.scalar.copy(adj_u8[slot][:, t, :], adj_in[:, t % 2, :]))
                for t in (2 * pair, 2 * pair + 1):
                    act.wait_ge(adj_turned.sem, adj_turned.at(b, t + 1))
                    adj_t_ready.raised_by(nc.scalar.copy(adj_t[slot][:, :, t * P:(t + 1) * P], turn[:, :, :]))

            def take_xt(b, layer):
                if layer == 0 and not (isinstance(b, int) and b == 0):
                    act.wait_ge(x_normed.sem, x_normed.at(b, 0))
                act.wait_ge(x_turned.sem, x_turned.at(b, layer + 1))
                xt_ready.raised_by(nc.scalar.copy(xt[:, :], low))

            def gat(b, slot, layer, between):
                l = layer - 1
                take_xt(b, layer)
                act.wait_ge(shifts_ready.sem, shifts_ready.at(b, layer))
                nc.scalar.activation(below[:, :], low, ACT.Relu, scale=NEG_SLOPE - 1.0, bias=shift[:, 0:1])
                bends_ready.raised_by(nc.scalar.activation(above[:, :], low, ACT.Relu, scale=1.0 - NEG_SLOPE,
                                                           bias=shift[:, 1:2]))
                act.wait_ge(z_psum.sem, z_psum.at(b, layer))
                z_ready.raised_by(nc.scalar.copy(values[:, :, 0:C], high_t))
                act.wait_ge(sum_psum.sem, sum_psum.at(b, layer))
                sum_ready.raised_by(nc.scalar.copy(value_sum[:, :], side[0:T, 512:512 + C + 1]))
                for j in range(T):
                    act.wait_ge(gat_logit.sem, gat_logit.at(b, l * T + j + 1))
                    gat_exp.raised_by(nc.scalar.activation(work[:, j % 2, :], work[:, j % 2, :], ACT.Exp,
                                                           scale=-1.0, bias=col_gap[:, j:j + 1]))
                between()
                act.wait_ge(elu_in.sem, elu_in.at(b, layer))
                elu_exp.raised_by(nc.scalar.activation(work[:, 0, :], work[:, 0, :], ACT.Exp))

            def graph(b, slot, in_loop):
                def point(n):
                    for ahead, pair in FEED.get(n, []):
                        if exists(b, ahead, B, in_loop):
                            feed(b + ahead, (slot + ahead) % 2, pair, ahead == 2)
                take_xt(b, 0)
                act.wait_ge(pooled_turned.sem, pooled_turned.at(b, 1))
                pooled_t_ready.raised_by(nc.scalar.copy(pooled_t, high))
                point(1)
                gat(b, slot, 1, lambda: point(2))
                point(3)
                gat(b, slot, 2, lambda: point(4))
                point(5)
                take_xt(b, 3)
                act.wait_ge(q_psum.sem, q_psum.at(b, 1))
                q_ready.raised_by(nc.scalar.mul(below[:, :], high, float(C) ** -0.5))
                act.wait_ge(xw_psum.sem, xw_psum.at(b, 1))
                xw_ready.raised_by(nc.scalar.copy(values[:, :, 0:C], low_t))
                for t in range(T + 1):
                    if t < T:
                        act.wait_ge(row_max.sem, row_max.at(b, t + 1))
                        if t >= 2:
                            act.wait_ge(att_turned.sem, att_turned.at(b, t - 1))
                        att_exp.raised_by(nc.scalar.activation(work[:, t % 2, :], (low, high)[t % 2], ACT.Exp,
                                                               bias=neg_max[:, t:t + 1]))
                    if t >= 1:
                        act.wait_ge(att_turned.sem, att_turned.at(b, t))
                        att_t_ready.raised_by(nc.scalar.copy(probs_t[:, :, (t - 1) * P:t * P], side_t))
                point(6)
                act.wait_ge(recip_ready.sem, recip_ready.at(b, 1))
                for step in range(2):
                    src = (low_t, high_t)[step]
                    for t in range(T):
                        if t % 4 == 0:
                            act.wait_ge(att_heads.sem, att_heads.at(b, 2 * step + t // 4 + 1))
                        att_tanh.raised_by(nc.scalar.activation(head[:, t, :], src[:, t, :], ACT.Tanh,
                                                                scale=recip[:, t:t + 1]))
                    if step == 0:
                        act.wait_ge(y_turned.sem, y_turned.at(b, 1))
                        y_ready.raised_by(nc.scalar.copy(xt[:, :], high))
                        act.wait_ge(xw_psum.sem, xw_psum.at(b, 2))
                        xw_ready.raised_by(nc.scalar.copy(values[:, :, 0:C], low_t))
                        point(7)
                point(8)

            act.wait_ge(consts, N_CONST)
            att_tanh.raised_by(nc.scalar.copy(ident_bf[:, :], ident[:, :]))
            nc.scalar.copy(group_key[:, :], group_key_i).then_inc(setup_done, 1)
            act.wait_ge(setup_psum, 1)
            for l in range(2):
                nc.scalar.copy(gat_wt[l][:, :], side[:, l * P:(l + 1) * P])
            nc.scalar.copy(score_bias[:, 0:1], side[:, 256:257])
            nc.scalar.mul(neg_score_bias[:, 0:1], side[:, 256:257], -1.0)
            nc.scalar.mul(score_bias[:, 1:2], side[:, 256:257], 0.0)
            nc.scalar.mul(neg_score_bias[:, 1:2], side[:, 256:257], 0.0).then_inc(setup_done, 1)
            act.wait_ge(setup_psum, 2)
            for l in range(2):
                last = nc.scalar.copy(gat_srow[l][:, :, :], high[:, l * 2 * P:(l + 1) * 2 * P].rearrange(
                    "p (h c) -> p h c", h=2))
            last.then_inc(setup_done, 1)

            for pair in range(PAIRS):
                feed(0, 0, pair, False)
            feed(1, 1, 0, False)
            with act.Fori(0, LOOPED // 2) as two:
                graph(two * 2, 0, True)
                graph(two * 2 + 1, 1, True)
            for b in range(LOOPED, B):
                graph(b, b % 2, False)

        @block.tensor
        def _(pe):
            def transposes(dst, src):
                for t in range(T):
                    last = nc.tensor.transpose(dst[:, t * P:(t + 1) * P], src[:, t, :], ident[:, :])
                return last

            def feed(b, slot, pair):
                for t in (2 * pair, 2 * pair + 1):
                    pe.wait_ge(adj_converted.sem, adj_converted.at(b, t + 1))
                    if not (isinstance(b, int) and b == 0 and t == 0):
                        pe.wait_ge(adj_t_ready.sem, adj_t_ready.at(b, t))
                    for j in range(T):
                        last = nc.tensor.transpose(turn[:, j, :], adj_bf[:, t % 2, j * P:(j + 1) * P],
                                                   ident_bf[:, :])
                    adj_turned.raised_by(last)
                if not (isinstance(b, int) and b == 0 and pair == 0):
                    pe.wait_ge(packed_read.sem, packed_read.at(b, pair))
                for t in (2 * pair, 2 * pair + 1):
                    pe.wait_ge(adj_t_ready.sem, adj_t_ready.at(b, t + 1))
                    for j in range(T):
                        last = nc.tensor.matmul(packed[:, t % 2, j * GP:(j + 1) * GP],
                                                adj_t[slot][:, j, t * P:(t + 1) * P], pack_w[:, :],
                                                start=True, stop=True)
                packed_ready.raised_by(last)

            def project(dst, w, bias_row):
                for t in range(T):
                    last = nc.tensor.matmul(dst[:, t, :], xt[:, t * P:(t + 1) * P], w, start=True,
                                            stop=bias_row is None)
                    if bias_row is not None:
                        last = nc.tensor.matmul(dst[:, t, :], ones[0:1, :], bias_row, start=False, stop=True)
                return last

            def turn_x(b, slot, layer):
                x_turned.raised_by(transposes(low, xs[slot]))
                pe.wait_ge(xt_ready.sem, xt_ready.at(b, layer + 1))

            def gat(b, slot, layer, between):
                l = layer - 1
                pe.wait_ge(x_normed.sem, x_normed.at(b, layer))
                turn_x(b, slot, layer)
                for t in range(T):
                    nc.tensor.matmul(side[:, t:t + 1], xt[:, t * P:(t + 1) * P], gat_srow[l][:, 1, 0:1],
                                     start=True, stop=True)
                for dst, h in ((high, 1), (low, 0)):
                    for half in halves:
                        last = nc.tensor.matmul(dst[:, half], gat_srow[l][:, h, :], xt[:, half],
                                                start=True, stop=True)
                scores_psum.raised_by(last)
                pe.wait_ge(shifts_ready.sem, shifts_ready.at(b, layer))
                z_psum.raised_by(project(high_t, gat_wt[0][:, :] if l == 0 else gat_w[1][:, :],
                                         b1_row[:, :] if l == 0 else None))
                pe.wait_ge(z_ready.sem, z_ready.at(b, layer))
                for j in range(T):
                    last = nc.tensor.matmul(side[0:T, 512:512 + C + 1], ones[:, 0:T], values[:, j, :],
                                            start=(j == 0), stop=(j == T - 1))
                sum_psum.raised_by(last)
                for j in range(T):
                    pe.wait_ge(gat_probs.sem, gat_probs.at(b, l * T + j + 1))
                    for t in range(T):
                        nc.tensor.matmul(heads[:, t, 0:C + 1], probs_t[:, j, t * P:(t + 1) * P], values[:, j, :],
                                         start=(j == 0 and t % 2 == 0), stop=False, skip_group_check=True)
                pe.wait_ge(sum_ready.sem, sum_ready.at(b, layer))
                for t in range(T):
                    last = nc.tensor.matmul(heads[:, t, 0:C + 1], zsel[:, t, :], value_sum[:, :],
                                            start=False, stop=True, skip_group_check=True)
                gat_heads.raised_by(last)
                between()

            def graph(b, slot, in_loop):
                def point(n):
                    for ahead, pair in FEED.get(n, []):
                        if exists(b, ahead, B, in_loop):
                            feed(b + ahead, (slot + ahead) % 2, pair)
                pe.wait_ge(x_loaded[slot].sem, x_loaded[slot].at(b, 2 - slot))
                if not (isinstance(b, int) and b == 0):
                    pe.wait_ge(att_tanh.sem, att_tanh.at(b, 0))
                x_turned.raised_by(transposes(low, xs[slot]))
                pe.wait_ge(rows_ready.sem, rows_ready.at(b, PAIRS))
                iso_turned.raised_by(nc.tensor.transpose(side[0:T, 0:P], isolated[slot][:, :], ident[:, :]))
                pe.wait_ge(rows_pooled.sem, rows_pooled.at(b, T))
                pooled_turned.raised_by(transposes(high, pooled))
                pe.wait_ge(xt_ready.sem, xt_ready.at(b, 1))
                pe.wait_ge(pooled_t_ready.sem, pooled_t_ready.at(b, 1))
                for t in range(T):
                    nodes = slice(t * P, (t + 1) * P)
                    nc.tensor.matmul(low_t[:, t, :], xt[:, nodes], w0_sb[:, 0, :], start=True, stop=False)
                    nc.tensor.matmul(low_t[:, t, :], pooled_t[:, nodes], w0_sb[:, 1, :], start=False, stop=False)
                    last = nc.tensor.matmul(low_t[:, t, :], ones[0:1, :], b0_row[:, :], start=False, stop=True)
                sage_psum.raised_by(last)
                point(1)
                pe.wait_ge(zsel_ready.sem, zsel_ready.at(b, 1))
                gat(b, slot, 1, lambda: point(2))
                point(3)
                gat(b, slot, 2, lambda: point(4))
                point(5)
                pe.wait_ge(x_normed.sem, x_normed.at(b, 3))
                turn_x(b, slot, 3)
                for half in halves:
                    last = nc.tensor.matmul(high[:, half], watt_sb[:, :], xt[:, half], start=True, stop=True)
                q_psum.raised_by(last)
                xw_psum.raised_by(project(low_t, w3_sb[0][:, :], b3_row[0][:, :]))
                pe.wait_ge(q_ready.sem, q_ready.at(b, 1))
                pe.wait_ge(xw_ready.sem, xw_ready.at(b, 1))
                for t in range(T + 1):
                    if t < T:
                        if t >= 2:
                            pe.wait_ge(att_exp.sem, att_exp.at(b, t - 1))
                        for half in halves:
                            last = nc.tensor.matmul((low, high)[t % 2][:, half], below[:, t * P:(t + 1) * P],
                                                    xt[:, half], start=True, stop=True)
                        logits_psum.raised_by(last)
                    if t >= 1:
                        pe.wait_ge(att_masked.sem, att_masked.at(b, t))
                        if t >= 2:
                            pe.wait_ge(att_t_ready.sem, att_t_ready.at(b, t - 1))
                        for m in range(T):
                            last = nc.tensor.transpose(side_t[:, m, :], work[:, (t - 1) % 2, m * P:(m + 1) * P],
                                                       ident[:, :])
                        att_turned.raised_by(last)
                point(6)
                pe.wait_ge(att_t_ready.sem, att_t_ready.at(b, T))
                for step in range(2):
                    for t in range(T):
                        for m in range(T):
                            last = nc.tensor.matmul((low_t, high_t)[step][:, t, :], probs_t[:, m, t * P:(t + 1) * P],
                                                    values[:, m, 0:C], start=(m == 0), stop=(m == T - 1))
                        if t % 4 == 3:
                            att_heads.raised_by(last)
                    if step == 0:
                        pe.wait_ge(att_tanh.sem, att_tanh.at(b, T))
                        y_turned.raised_by(transposes(high, head))
                        pe.wait_ge(y_ready.sem, y_ready.at(b, 1))
                        xw_psum.raised_by(project(low_t, w3_sb[1][:, :], b3_row[1][:, :]))
                        pe.wait_ge(xw_ready.sem, xw_ready.at(b, 2))
                        point(7)
                point(8)

            pe.wait_ge(weights, WEIGHTS_IN)
            pe.wait_ge(consts, N_CONST)
            pe.wait_ge(reps_ready, 1)
            for l in range(2):
                nc.tensor.transpose(side[:, l * P:(l + 1) * P], gat_w[l][:, :], ident[:, :])
            for h in range(2):
                last = nc.tensor.matmul(side[:, 256:257], b1_rep, gat_a[0][:, h:h + 1],
                                        start=(h == 0), stop=(h == 1))
            last.then_inc(setup_psum, 1)
            pe.wait_ge(setup_done, 2)
            for l in range(2):
                w = gat_w[0] if l == 0 else gat_wt[1]
                for h in range(2):
                    last = nc.tensor.matmul(high[:, (2 * l + h) * P:(2 * l + h + 1) * P], w[:, :],
                                            gat_arep[l][:, h, :], start=True, stop=True)
            last.then_inc(setup_psum, 1)
            pe.wait_ge(setup_done, 3)

            for pair in range(PAIRS):
                feed(0, 0, pair)
            feed(1, 1, 0)
            with pe.Fori(0, LOOPED // 2) as two:
                graph(two * 2, 0, True)
                graph(two * 2 + 1, 1, True)
            for b in range(LOOPED, B):
                graph(b, b % 2, False)

        @block.vector
        def _(dve):
            steps = Steps(dve)
            done, settle, link = steps.done, steps.settle, steps.link

            def bc(ap, shape):
                return ap.to_broadcast(shape)

            def top_32(dst, src):
                for r in range(TOP // 8):
                    if r:
                        link(nc.vector.match_replace(out=src, in_to_replace=dst[:, 8 * r - 8:8 * r],
                                                     in_values=src, imm_value=0.0))
                    link(nc.vector.max(dst[:, 8 * r:8 * r + 8], src))

            def search(b, slot, pair):
                two = slice(2 * pair, 2 * pair + 2)
                dve.wait_ge(packed_ready.sem, packed_ready.at(b, pair + 1))
                nc.vector.tensor_scalar(isolated[slot][:, two], degree[slot][:, two], 0.0, None, ALU.is_equal)
                nc.vector.tensor_scalar(connected[slot][:, two], degree[slot][:, two], 0.0, None, ALU.is_gt)
                nc.vector.tensor_scalar(pool_floor[slot][:, two], degree[slot][:, two], float(SAMPLES), LOWEST,
                                        ALU.is_gt, ALU.mult)
                for i in range(2):
                    done(nc.vector.scalar_tensor_tensor(out=keys[:, i, :], in0=packed[:, i, :], scalar=0.0,
                                                        in1=group_key[:, :], op0=ALU.is_gt, op1=ALU.mult))
                settle()
                packed_read.raised_by(nc.vector.tensor_tensor(keys[:, :, :], keys[:, :, :], packed[:, :, :], ALU.add))
                settle()
                for i in range(2):
                    top_32(top_keys[:, i, :], keys[:, i, :])
                link(nc.vector.tensor_copy(top_int[:, :, :], top_keys[:, :, :]))
                done(nc.vector.tensor_scalar(top_base[:, :, :], top_int[:, :, :], GROUP, 2,
                                             ALU.logical_shift_right, ALU.logical_shift_left))
                for bit in range(GROUP):
                    done(nc.vector.tensor_scalar(top_bit[:, bit, :, :], top_int[:, :, :], bit, 1,
                                                 ALU.logical_shift_right, ALU.bitwise_and))
                settle()
                for bit in range(GROUP):
                    done(nc.vector.scalar_tensor_tensor(out=members[:, :, bit, :], in0=top_base[:, :, :],
                                                        scalar=float(bit), in1=top_bit[:, bit, :, :],
                                                        op0=ALU.subtract, op1=ALU.mult))
                settle()
                for i in range(2):
                    top_32(top_members[:, i, :], members[:, i, :, :].rearrange("p g k -> p (g k)"))
                first = top_members[:, :, 0:SAMPLES]
                link(nc.vector.scalar_tensor_tensor(out=missing[:, :, :], in0=first, scalar=0.0,
                                                    in1=bc(top_members[:, :, 0:1], [P, 2, SAMPLES]),
                                                    op0=ALU.is_equal, op1=ALU.mult))
                link(nc.vector.tensor_tensor(row_f[:, :, :], missing[:, :, :], first, ALU.add))
                link(nc.vector.tensor_scalar(row_f[:, :, :], row_f[:, :, :], -1.0, float(N), ALU.mult, ALU.add))
                rows_ready.raised_by(nc.vector.tensor_scalar(rows[:, two, :], row_f[:, :, :], float(N - 1),
                                                             row_base[:, 0:1], ALU.min, ALU.add))
                if pair == PAIRS - 1:
                    dve.wait_ge(rows_ready.sem, rows_ready.at(b, PAIRS))
                    link(nc.vector.tensor_scalar(row_base[:, :], row_base[:, :], float(N), None, ALU.add))

            def pool_tile(b, slot, t):
                ring = rows_gathered[t % RING]
                dve.wait_ge(ring.sem, ring.at(b, (t // RING + 1) * SAMPLES))
                if t == 0 and not (isinstance(b, int) and b == 0):
                    dve.wait_ge(pooled_turned.sem, pooled_turned.at(b, 0))
                link(nc.vector.tensor_reduce(
                    pooled[:, t, :], gathered[:, t % RING, :].rearrange("p (k c) -> p c k", k=SAMPLES), AX.X, ALU.max))
                rows_pooled.raised_by(nc.vector.tensor_scalar(
                    pooled[:, t, :], pooled[:, t, :], connected[slot][:, t:t + 1], pool_floor[slot][:, t:t + 1],
                    ALU.mult, ALU.max))

            def layer_norm(slot):
                for t in range(T):
                    done(nc.vector.bn_stats(stats[:, t, :], xs[slot][:, t, :]))
                settle()
                for t in range(T):
                    done(nc.vector.bn_aggr(moments[:, t, :], stats[:, t, :]))
                settle()
                link(nc.vector.tensor_scalar(spread[:, :], moments[:, :, 1], EPS, None, ALU.add))
                link(nc.vector.tensor_scalar(guess[:, :], spread[:, :].bitcast(I32), 1, None,
                                             ALU.logical_shift_right))
                link(nc.vector.tensor_scalar(rstd[:, :].bitcast(I32), guess[:, :], -1.0, RSQRT_GUESS,
                                             ALU.mult, ALU.add))
                for _ in range(3):
                    link(nc.vector.tensor_tensor(error[:, :], rstd[:, :], rstd[:, :], ALU.mult))
                    link(nc.vector.scalar_tensor_tensor(out=error[:, :], in0=error[:, :], scalar=-0.5,
                                                        in1=spread[:, :], op0=ALU.mult, op1=ALU.mult))
                    link(nc.vector.scalar_tensor_tensor(out=rstd[:, :], in0=error[:, :], scalar=1.5,
                                                        in1=rstd[:, :], op0=ALU.add, op1=ALU.mult))
                for t in range(T):
                    last = nc.vector.tensor_scalar(xs[slot][:, t, :], xs[slot][:, t, :], moments[:, t, 0:1],
                                                   rstd[:, t:t + 1], ALU.subtract, ALU.mult)
                x_normed.raised_by(last)

            def gat(b, slot, layer, between):
                l = layer - 1
                flat = xs[slot][:, :, :].rearrange("p t c -> p (t c)")
                flat_head = head[:, :, :].rearrange("p t c -> p (t c)")
                dve.wait_ge(scores_psum.sem, scores_psum.at(b, layer))
                done(nc.vector.tensor_reduce(top_score[:, :], high, AX.X, ALU.max))
                done(nc.vector.tensor_scalar(col_score[:, :], side[:, 0:T], score_bias[:, l:l + 1], None, ALU.add))
                settle()
                link(nc.vector.tensor_scalar(neg_top[:, :], top_score[:, :], -1.0, neg_score_bias[:, l:l + 1],
                                             ALU.mult, ALU.add))
                done(nc.vector.tensor_scalar(shift[:, 0:1], neg_top[:, :], 1.0 - NEG_SLOPE, None, ALU.mult))
                done(nc.vector.tensor_scalar(shift[:, 1:2], neg_top[:, :], NEG_SLOPE - 1.0, None, ALU.mult))
                link(nc.vector.tensor_scalar(col_gap[:, :], col_score[:, :], neg_top[:, 0:1], None, ALU.add))
                shifts_ready.raised_by(nc.vector.tensor_scalar(col_gap8[:, :], col_gap[:, :], 1.0 - NEG_SLOPE, None,
                                                               ALU.mult))
                dve.wait_ge(shifts_ready.sem, shifts_ready.at(b, layer))
                dve.wait_ge(bends_ready.sem, bends_ready.at(b, layer))
                for j in range(T + 1):
                    if j < T:
                        gat_logit.raised_by(nc.vector.scalar_tensor_tensor(
                            out=work[:, j % 2, :], in0=above[:, :], scalar=col_gap8[:, j:j + 1], in1=below[:, :],
                            op0=ALU.add, op1=ALU.min))
                    if j >= 1:
                        dve.wait_ge(gat_exp.sem, gat_exp.at(b, l * T + j))
                        gat_probs.raised_by(nc.vector.tensor_tensor(
                            probs_t[:, j - 1, :], work[:, (j - 1) % 2, :], adj_t[slot][:, j - 1, :], ALU.mult))
                        settle()
                between()
                dve.wait_ge(gat_heads.sem, gat_heads.at(b, layer))
                link(nc.vector.reciprocal(recip[:, :], heads[:, :, C]))
                link(nc.vector.tensor_tensor(head[:, :, :], heads[:, :, 0:C],
                                             bc(recip[:, :].rearrange("p (t a) -> p t a", a=1), [P, T, C]), ALU.mult))
                elu_in.raised_by(nc.vector.tensor_scalar(work[:, 0, :], flat_head, 0.0, None, ALU.min))
                link(nc.vector.scalar_tensor_tensor(out=flat, in0=flat_head, scalar=0.0, in1=flat,
                                                    op0=ALU.max, op1=ALU.add))
                dve.wait_ge(elu_exp.sem, elu_exp.at(b, layer))
                link(nc.vector.scalar_tensor_tensor(out=flat, in0=work[:, 0, :], scalar=-1.0, in1=flat,
                                                    op0=ALU.add, op1=ALU.add))
                layer_norm(slot)

            def graph(b, slot, in_loop):
                def point(n):
                    for kind, ahead, i in SIDE.get(n, []):
                        if exists(b, ahead, B, in_loop):
                            (search if kind == "search" else pool_tile)(b + ahead, (slot + ahead) % 2, i)
                flat = xs[slot][:, :, :].rearrange("p t c -> p (t c)")
                dve.wait_ge(iso_turned.sem, iso_turned.at(b, 1))
                zsel_ready.raised_by(nc.vector.tensor_tensor(
                    zsel[:, :, :], bc(ident[0:T, 0:T].rearrange("p (t a) -> p t a", a=1), [T, T, P]),
                    side[0:T, 0:P].unsqueeze(1).broadcast_to([T, T, P]), ALU.mult))
                dve.wait_ge(sage_psum.sem, sage_psum.at(b, 1))
                link(nc.vector.scalar_tensor_tensor(out=flat, in0=low, scalar=0.0, in1=flat,
                                                    op0=ALU.max, op1=ALU.add))
                layer_norm(slot)
                point(1)
                gat(b, slot, 1, lambda: point(2))
                point(3)
                gat(b, slot, 2, lambda: point(4))
                point(5)
                for t in range(T + 1):
                    if t < T:
                        dve.wait_ge(logits_psum.sem, logits_psum.at(b, t + 1))
                        row_max.raised_by(nc.vector.tensor_reduce(neg_max[:, t:t + 1], (low, high)[t % 2], AX.X,
                                                                  ALU.max, negate=True))
                    if t >= 1:
                        dve.wait_ge(att_exp.sem, att_exp.at(b, t))
                        att_masked.raised_by(nc.vector.scalar_tensor_tensor(
                            out=work[:, (t - 1) % 2, :], in0=adj_u8[slot][:, t - 1, :],
                            scalar=isolated[slot][:, t - 1:t], in1=work[:, (t - 1) % 2, :],
                            op0=ALU.add, op1=ALU.mult, accum_out=row_sum[:, t - 1:t]))
                        settle()
                dve.wait_ge(att_masked.sem, att_masked.at(b, T))
                recip_ready.raised_by(nc.vector.reciprocal(recip[:, :], row_sum[:, :]))
                point(6)
                point(7)
                dve.wait_ge(att_tanh.sem, att_tanh.at(b, 2 * T))
                link(nc.vector.tensor_tensor(flat, flat, head[:, :, :].rearrange("p t c -> p (t c)"), ALU.add))
                layer_norm(slot)
                point(8)

            dve.wait_ge(weights, WEIGHTS_IN)
            for l in range(2):
                for h in range(2):
                    nc.vector.tensor_copy(gat_arep[l][:, h, :], bc(gat_a[l][:, h:h + 1], [P, P]))
            nc.vector.tensor_copy(b1_rep, bc(b1_col[:, 0:1], [P, P])).then_inc(reps_ready, 1)
            x_normed.raised_by(nc.vector.memset(row_base[:, :], 0.0))
            settle()
            dve.wait_ge(setup_done, 3)

            for pair in range(PAIRS):
                search(0, 0, pair)
            for t in range(T):
                if t == T - 2:
                    search(1, 1, 0)
                pool_tile(0, 0, t)
            with dve.Fori(0, LOOPED // 2) as two:
                graph(two * 2, 0, True)
                graph(two * 2 + 1, 1, True)
            for b in range(LOOPED, B):
                graph(b, b % 2, False)


_INS = ['x', 'adj', 'L0_gnn_W', 'L0_gnn_b', 'L1_gnn_W', 'L1_gnn_b', 'L1_gnn_a', 'L2_gnn_W', 'L2_gnn_a',
        'L3_gnn_att_W', 'L3_gnn_W0', 'L3_gnn_b0', 'L3_gnn_W1', 'L3_gnn_b1']


def kernel(**inputs):
    import numpy as _np
    import concourse.bacc as _bacc
    from concourse import mybir as _mybir
    from concourse.bass_utils import run_bass_kernel_spmd as _run

    nc = _bacc.Bacc("TRN2", target_bir_lowering=False, num_devices=1)
    arrays, args = {}, []
    for name in _INS:
        a = _np.ascontiguousarray(inputs[name])
        arrays[f"in_{name}_dram"] = a
        args.append(nc.dram_tensor(f"in_{name}_dram", a.shape, _mybir.dt.from_np(a.dtype), kind="ExternalInput").ap())
    out = nc.dram_tensor("out_0_dram", inputs["x"].shape, _mybir.dt.float32, kind="ExternalOutput").ap()
    build_graph_layers(nc, *args, out)
    r = _run(nc, [arrays], core_ids=[0])
    return r.results[0]["out_0_dram"]
```

```python
import concourse.bass as bass
from concourse import mybir
from contextlib import ExitStack

F32 = mybir.dt.float32
BF16 = mybir.dt.bfloat16
I32 = mybir.dt.int32
U32 = mybir.dt.uint32
U8 = mybir.dt.uint8
ALU = mybir.AluOpType
ACT = mybir.ActivationFunctionType
AX = mybir.AxisListType

P = 128
SAMPLES = 25
NEG_SLOPE = 0.2
EPS = 1e-5
GROUP = 4
TOP = 32
RING = 4
LOWEST = -3.0e38
RSQRT_GUESS = float(0x5f3759df)


class Signal:

    def __init__(self, ctx, nc, name, per, unit=1, ahead=0):
        self.sem = ctx.enter_context(nc.semaphore(name))
        self.per, self.unit, self.ahead = per, unit, ahead

    def at(self, b, k):
        return b * (self.per * self.unit) + (k + self.ahead) * self.unit

    def raised_by(self, instruction):
        return instruction.then_inc(self.sem, self.unit)


class Steps:

    def __init__(self, eng):
        self.settle = eng.drain

    def done(self, instruction):
        pass

    def link(self, instruction):
        self.settle()


FEED = {0: (1, 2), 1: (1, 3), 2: (2, 0), 3: (2, 1)}
SIDE = {"layer 0": [("keys", 1, 1), ("members", 1, 1)],
        "gat 1": [("keys", 1, 2)],
        "gat 1 heads": [("pool", 1, 0), ("members", 1, 2)],
        "gat 2": [("keys", 1, 3), ("pool", 1, 1)],
        "gat 2 heads": [("members", 1, 3), ("pool", 1, 2)],
        "attention": [("pool", 1, 3), ("pool", 1, 4)],
        "steps": [("keys", 2, 0), ("members", 2, 0), ("pool", 1, 5)],
        "end": [("pool", 1, 6), ("pool", 1, 7)]}


def exists(b, ahead, graphs, in_loop):
    return in_loop or b + ahead < graphs


def build_graph_layers(nc, x, adj, w0, b0, w1, b1, a1, w2, a2, watt, w3a, b3a, w3b, b3b, out):
    B, N, C = x.shape
    T = N // P
    PAIRS = T // 2
    G = N // GROUP
    GP = P // GROUP
    LOOPED = B - 2
    assert C == P and T % RING == 0 and LOOPED % 2 == 0

    x_rows = x.rearrange("b n c -> (b n) c")
    x_tiles = x.rearrange("b (t p) c -> b p t c", p=P)
    out_tiles = out.rearrange("b (t p) c -> b p t c", p=P)
    adj_tiles = adj.rearrange("b (t p) m -> b t p m", p=P)

    with ExitStack() as ctx:
        def sb(name, shape, dt=F32):
            return ctx.enter_context(nc.sbuf_tensor(name, shape, dt))

        def ps(name, shape, dt=F32):
            return ctx.enter_context(nc.psum_tensor(name, shape, dt))

        def signal(name, per, unit=1, ahead=0):
            return Signal(ctx, nc, name, per, unit, ahead)

        ident = sb("ident", [P, P])
        ident_bf = sb("ident_bf", [P, P], BF16)
        ones = sb("ones", [P, P])
        pack_w = sb("pack_w", [P, GP], BF16)
        group_key = sb("group_key", [P, G])
        w0_sb = sb("w0_sb", [P, 2, P])
        b0_row = sb("b0_row", [1, P])
        gat_w = [sb(f"gat_w{l}", [P, P]) for l in range(2)]
        gat_wt = [sb(f"gat_wt{l}", [P, P]) for l in range(2)]
        gat_a = [sb(f"gat_a{l}", [P, 2]) for l in range(2)]
        gat_srow = [sb(f"gat_srow{l}", [P, 2, P]) for l in range(2)]
        b1_row = sb("b1_row", [1, P])
        b1_col = sb("b1_col", [P, 1])
        score_bias = sb("score_bias", [P, 2])
        neg_score_bias = sb("neg_score_bias", [P, 2])
        watt_sb = sb("watt_sb", [P, P])
        w3_sb = [sb(f"w3_sb{l}", [P, P]) for l in range(2)]
        b3_row = [sb(f"b3_row{l}", [1, P]) for l in range(2)]

        adj_in = sb("adj_in", [P, 2, N], I32)
        adj_bf = sb("adj_bf", [P, 2, N], BF16)
        adj_u8 = [sb(f"adj_u8{i}", [P, T, N], U8) for i in range(2)]
        adj_t = [sb(f"adj_t{i}", [P, T, N], BF16) for i in range(2)]
        degree = [sb(f"degree{i}", [P, T]) for i in range(2)]
        isolated = [sb(f"isolated{i}", [P, T]) for i in range(2)]
        connected = [sb(f"connected{i}", [P, T]) for i in range(2)]
        pool_floor = [sb(f"pool_floor{i}", [P, T]) for i in range(2)]
        keys = sb("keys", [P, 2, G])
        top_keys = sb("top_keys", [P, 2, TOP])
        top_int = sb("top_int", [P, 2, TOP], I32)
        top_base = sb("top_base", [P, 2, TOP], I32)
        top_bit = sb("top_bit", [P, GROUP, 2, TOP], I32)
        members = sb("members", [P, 2, GROUP, TOP])
        top_members = sb("top_members", [P, 2, TOP])
        missing = sb("missing", [P, 2, SAMPLES])
        row_base = sb("row_base", [P, 1])
        row_f = sb("row_f", [P, 2, SAMPLES])
        rows = sb("rows", [P, T, SAMPLES], U32)
        gathered = sb("gathered", [P, RING, SAMPLES * C])
        pooled = sb("pooled", [P, T, C])
        xs = [sb(f"xs{i}", [P, T, C]) for i in range(2)]
        xt = sb("xt", [P, N])
        row_gain = sb("row_gain", [P, N])
        queries = row_gain
        work = sb("work", [P, 3, N])
        relu_part = work[:, 0, :].rearrange("p (t c) -> p t c", t=T)
        exp_part = work[:, 1, :].rearrange("p (t c) -> p t c", t=T)
        probs_t = sb("probs_t", [P, T, N])
        pooled_t = probs_t[:, 0, :]
        gat_arep = [work[:, 0, l * 2 * P:(l + 1) * 2 * P].rearrange("p (h c) -> p h c", h=2) for l in range(2)]
        b1_rep = work[:, 1, 0:P]
        group_key_i = row_gain[:, 0:G].bitcast(I32)
        values = sb("values", [P, T, C + 1])
        head = xt[:, :].rearrange("p (t c) -> p t c", t=T)
        iso_row = sb("iso_row", [1, N])
        x_sum = sb("x_sum", [P, 1])
        value_sum = sb("value_sum", [1, C + 1])
        n_nodes = sb("n_nodes", [1, 1])
        lane_top = sb("lane_top", [P, 2])
        both_top = sb("both_top", [2, 1])
        both_diag = sb("both_diag", [2, 2])
        neg_top = sb("neg_top", [P, 1])
        crest = sb("crest", [P, 1])
        row_shift = sb("row_shift", [P, 1])
        col_shift = sb("col_shift", [P, 1])
        col_gap = sb("col_gap", [P, T])
        col_gain = sb("col_gain", [P, T])
        recip = sb("recip", [P, T])
        neg_max = sb("neg_max", [P, T])
        row_sum = sb("row_sum", [P, T])
        stats = sb("stats", [P, T, 6])
        moments = sb("moments", [P, T, 2])
        rstd = sb("rstd", [P, T])
        spread = sb("spread", [P, T])
        guess = sb("guess", [P, T], I32)
        error = sb("error", [P, T])
        offset = sb("offset", [P, T])

        turn = ps("turn", [P, T, P], BF16)
        packed = ps("packed", [P, 2, G])
        big = ps("big", [P, 4 * 512])
        side = ps("side", [P, N])
        low, high = big[:, 0:N], big[:, N:2 * N]
        low_t = low.rearrange("p (t c) -> p t c", t=T)
        high_t = high.rearrange("p (t c) -> p t c", t=T)
        heads = big[:, :].rearrange("p (t c) -> p t c", t=T)
        side_t = side[:, :].rearrange("p (t c) -> p t c", t=T)
        halves = [slice(0, 512), slice(512, 1024)]

        weights = ctx.enter_context(nc.semaphore("weights"))
        consts = ctx.enter_context(nc.semaphore("consts"))
        reps_ready = ctx.enter_context(nc.semaphore("reps_ready"))
        setup_psum = ctx.enter_context(nc.semaphore("setup_psum"))
        setup_done = ctx.enter_context(nc.semaphore("setup_done"))
        adj_loaded = [signal(f"adj_loaded{i}", T // 2, 16) for i in range(2)]
        x_loaded = [signal(f"x_loaded{i}", 1, 8) for i in range(2)]
        out_stored = signal("out_stored", 1, 16, ahead=1)
        adj_converted = signal("adj_converted", T)
        adj_narrowed = signal("adj_narrowed", T)
        adj_turned = signal("adj_turned", T)
        adj_t_ready = signal("adj_t_ready", T)
        packed_ready = signal("packed_ready", PAIRS)
        packed_read = signal("packed_read", PAIRS)
        rows_ready = signal("rows_ready", PAIRS)
        rows_gathered = [signal(f"rows_gathered{i}", T // RING * SAMPLES, 16) for i in range(RING)]
        gathers_begun = ctx.enter_context(nc.semaphore("gathers_begun"))
        rows_pooled = signal("rows_pooled", T)
        pooled_turned = signal("pooled_turned", 2)
        pooled_t_ready = signal("pooled_t_ready", 2)
        x_turned = signal("x_turned", 4)
        xt_ready = signal("xt_ready", 4)
        sage_psum = signal("sage_psum", 2)
        iso_turned = signal("iso_turned", 1)
        iso_ready = signal("iso_ready", 1)
        norm_scale = signal("norm_scale", 4)
        x_normed = signal("x_normed", 4, ahead=1)
        x_normed2 = signal("x_normed2", 4)
        cols_psum = signal("cols_psum", 2)
        lanes_ready = signal("lanes_ready", 2)
        lanes_turned = signal("lanes_turned", 2)
        tops_ready = signal("tops_ready", 2)
        tops_spread = signal("tops_spread", 2)
        row_psum = signal("row_psum", 2)
        shifts_ready = signal("shifts_ready", 2)
        row_gain_ready = signal("row_gain_ready", 2)
        value_gain_ready = signal("value_gain_ready", 2)
        z_psum = signal("z_psum", 2)
        z_ready = signal("z_ready", 2)
        sum_psum = signal("sum_psum", 2)
        sum_ready = signal("sum_ready", 2)
        gat_probs = signal("gat_probs", 2 * T)
        gat_heads = signal("gat_heads", 2 * T // 2)
        gat_recip = signal("gat_recip", 2 * T // 2)
        elu_ready = signal("elu_ready", 4)
        q_psum = signal("q_psum", 1)
        q_ready = signal("q_ready", 1)
        xw_psum = signal("xw_psum", 2)
        xw_ready = signal("xw_ready", 2)
        logits_psum = signal("logits_psum", T)
        row_max = signal("row_max", T)
        att_exp = signal("att_exp", T)
        att_masked = signal("att_masked", T)
        att_turned = signal("att_turned", T)
        att_t_ready = signal("att_t_ready", T)
        recip_ready = signal("recip_ready", 1)
        att_heads = signal("att_heads", 4)
        att_tanh = signal("att_tanh", 2 * T, ahead=1)
        y_turned = signal("y_turned", 1)
        y_ready = signal("y_ready", 1)

        block = ctx.enter_context(nc.Block())
        N_CONST = 7 + GROUP
        loads = [(w0_sb[:, :, :], w0.rearrange("(h p) o -> p h o", p=P)),
                 (b0_row[:, :], b0.rearrange("(a c) -> a c", a=1)),
                 (gat_w[0][:, :], w1), (gat_w[1][:, :], w2),
                 (gat_a[0][:, :], a1.rearrange("(h p) -> p h", p=P)),
                 (gat_a[1][:, :], a2.rearrange("(h p) a -> p (h a)", p=P)),
                 (b1_row[:, :], b1.rearrange("(a c) -> a c", a=1)),
                 (b1_col[:, :], b1.rearrange("(p a) -> p a", a=1)),
                 (watt_sb[:, :], watt), (w3_sb[0][:, :], w3a), (w3_sb[1][:, :], w3b),
                 (b3_row[0][:, :], b3a.rearrange("(a c) -> a c", a=1)),
                 (b3_row[1][:, :], b3b.rearrange("(a c) -> a c", a=1))]
        WEIGHTS_IN = 16 * len(loads)

        @block.sync
        def _(sp):
            def load_adj(b, t):
                if not (isinstance(b, int) and b == 0 and t < 2):
                    sp.wait_ge(adj_narrowed.sem, adj_narrowed.at(b, t - 1))
                adj_loaded[t % 2].raised_by(sp.dma_start(adj_in[:, t % 2, :], adj_tiles[b, t]))

            def load_x(b, slot):
                if not (isinstance(b, int) and b < 2):
                    sp.wait_ge(out_stored.sem, out_stored.at(b - 1, 0))
                sp.dma_start(xs[slot][:, :, :], x_tiles[b]).then_inc(x_loaded[slot].sem, 16)

            def graph(b, slot, in_loop):
                if exists(b, 1, B, in_loop):
                    load_x(b + 1, 1 - slot)
                    for t in range(6, T):
                        load_adj(b + 1, t)
                if exists(b, 2, B, in_loop):
                    for t in range(6):
                        load_adj(b + 2, t)
                sp.wait_ge(x_normed2.sem, x_normed2.at(b, 4))
                out_stored.raised_by(sp.dma_start(out_tiles[b], xs[slot][:, :, :]))

            sp.sem_inc(out_stored.sem, out_stored.unit)
            for t in range(2):
                load_adj(0, t)
            for dst, src in loads:
                with nc.allow_non_contiguous_dma(reason="small weights"):
                    sp.dma_start(dst, src).then_inc(weights, 16)
            for t in range(2, T):
                load_adj(0, t)
            load_x(0, 0)
            for t in range(6):
                load_adj(1, t)
            with sp.Fori(0, LOOPED // 2) as two:
                graph(two * 2, 0, True)
                graph(two * 2 + 1, 1, True)
            for b in range(LOOPED, B):
                graph(b, b % 2, False)
            sp.wait_ge(out_stored.sem, out_stored.at(B, 0))

        @block.gpsimd
        def _(pool):
            nc.gpsimd.memset(ident[:, :], 0.0).then_inc(consts, 1)
            nc.gpsimd.memset(pack_w[:, :], 0.0).then_inc(consts, 1)
            nc.gpsimd.memset(ones[:, :], 1.0).then_inc(consts, 1)
            nc.gpsimd.iota(group_key_i, pattern=[[-(1 << GROUP), G]], base=G << GROUP,
                           channel_multiplier=0).then_inc(consts, 1)
            pool.wait_ge(consts, 4)
            nc.gpsimd.affine_select(out=ident[:, :], in_=ident[:, :], compare_op=ALU.not_equal, fill=1.0,
                                    base=0, pattern=[[-1, P]], channel_multiplier=1).then_inc(consts, 1)
            for bit in range(GROUP):
                nc.gpsimd.affine_select(out=pack_w[:, :], in_=pack_w[:, :], compare_op=ALU.not_equal,
                                        fill=float(1 << bit), base=bit, pattern=[[GROUP, GP]],
                                        channel_multiplier=-1).then_inc(consts, 1)
                pool.wait_ge(consts, 6 + bit)
            nc.gpsimd.memset(value_sum[:, C:C + 1], float(N)).then_inc(consts, 1)
            nc.gpsimd.memset(n_nodes[:, :], float(N)).then_inc(consts, 1)

            def gather(b, t):
                if t % 2 == 0:
                    pool.wait_ge(rows_ready.sem, rows_ready.at(b, t // 2 + 1))
                if not (isinstance(b, int) and b == 0 and t < RING):
                    pool.wait_ge(rows_pooled.sem, rows_pooled.at(b, t - RING + 1))
                pool.sem_inc(gathers_begun, 1)
                for k in range(SAMPLES):
                    rows_gathered[t % RING].raised_by(pool.indirect_dma_start(
                        out=gathered[:, t % RING, k * C:(k + 1) * C], out_offset=None, in_=x_rows,
                        in_offset=bass.IndirectOffsetOnAxis(ap=rows[:, t, k:k + 1], axis=0),
                        bounds_check=B * N - 1, oob_is_err=False))

            for t in range(T):
                gather(0, t)
            with pool.Fori(1, B) as b:
                for t in range(T):
                    gather(b, t)

        @block.scalar
        def _(act):
            def convert(b, slot, pair, reused=False):
                if pair == 0 and reused:
                    act.wait_ge(att_masked.sem, att_masked.at(b - 2, T))
                for t in (2 * pair, 2 * pair + 1):
                    act.wait_ge(adj_loaded[t % 2].sem, adj_loaded[t % 2].at(b, t // 2 + 1))
                    adj_converted.raised_by(nc.scalar.activation(
                        adj_bf[:, t % 2, :], adj_in[:, t % 2, :], ACT.Copy,
                        accum_out=degree[slot][:, t:t + 1]))
                    adj_narrowed.raised_by(nc.scalar.copy(adj_u8[slot][:, t, :], adj_in[:, t % 2, :]))

            def take_turned(b, slot, t):
                act.wait_ge(adj_turned.sem, adj_turned.at(b, t + 1))
                adj_t_ready.raised_by(nc.scalar.copy(adj_t[slot][:, :, t * P:(t + 1) * P], turn[:, :, :]))

            def feed(b, slot, layer, part, in_loop):
                ahead, pair = FEED[layer]
                if exists(b, ahead, B, in_loop):
                    if part == 0:
                        convert(b + ahead, (slot + ahead) % 2, pair, ahead == 2)
                    else:
                        for t in (2 * pair, 2 * pair + 1):
                            take_turned(b + ahead, (slot + ahead) % 2, t)

            def take_xt(b, layer):
                if layer == 0 and not (isinstance(b, int) and b == 0):
                    act.wait_ge(x_normed.sem, x_normed.at(b, 0))
                act.wait_ge(x_turned.sem, x_turned.at(b, layer + 1))
                xt_ready.raised_by(nc.scalar.activation(xt[:, :], low, ACT.Copy, accum_out=x_sum[:, 0:1]))

            def norm_half(b, slot, layer):
                act.wait_ge(norm_scale.sem, norm_scale.at(b, layer + 1))
                for t in range(T // 2, T):
                    if layer == 3 and t == T - 1:
                        act.wait_ge(x_normed.sem, x_normed.at(b, 4))
                    last = nc.scalar.activation(xs[slot][:, t, :], xs[slot][:, t, :], ACT.Identity,
                                                scale=rstd[:, t:t + 1], bias=offset[:, t:t + 1])
                x_normed2.raised_by(last)

            def gat(b, slot, layer, in_loop):
                l = layer - 1
                take_xt(b, layer)
                act.wait_ge(sum_psum.sem, sum_psum.at(b, layer))
                sum_ready.raised_by(nc.scalar.copy(value_sum[:, 0:C], side[0:1, 512:512 + C]))
                act.wait_ge(shifts_ready.sem, shifts_ready.at(b, layer))
                act.wait_ge(row_psum.sem, row_psum.at(b, layer))
                nc.scalar.activation(col_gain[:, :], col_gap[:, :], ACT.Exp, scale=NEG_SLOPE - 1.0,
                                     bias=col_shift[:, 0:1])
                row_gain_ready.raised_by(nc.scalar.activation(row_gain[:, :], low, ACT.Exp, scale=1.0 - NEG_SLOPE,
                                                              bias=row_shift[:, 0:1]))
                value_gain_ready.raised_by(nc.scalar.activation(
                    values[:, :, C:C + 1].rearrange("p t a -> p (t a)"), col_gap[:, :], ACT.Exp))
                act.wait_ge(value_gain_ready.sem, value_gain_ready.at(b, layer))
                act.wait_ge(z_psum.sem, z_psum.at(b, layer))
                for t in range(T):
                    last = nc.scalar.activation(values[:, t, 0:C], high_t[:, t, :], ACT.Copy,
                                                scale=values[:, t, C:C + 1])
                z_ready.raised_by(last)
                if layer == 1:
                    feed(b, slot, layer, 0, in_loop)
                for t in range(T):
                    if t % 2 == 0:
                        act.wait_ge(gat_recip.sem, gat_recip.at(b, (l * T + t) // 2 + 1))
                    nc.scalar.activation(relu_part[:, t, :], heads[:, t, 0:C], ACT.Relu, scale=recip[:, t:t + 1])
                    last = nc.scalar.activation(exp_part[:, t, :], heads[:, t, 0:C], ACT.Exp,
                                                scale=recip[:, t:t + 1])
                    if t % 4 == 3:
                        elu_ready.raised_by(last)
                if layer == 1:
                    feed(b, slot, layer, 1, in_loop)
                norm_half(b, slot, layer)

            def graph(b, slot, in_loop):
                take_xt(b, 0)
                act.wait_ge(iso_turned.sem, iso_turned.at(b, 1))
                iso_ready.raised_by(nc.scalar.copy(iso_row[:, :], side[0:1, :]))
                for h in range(2):
                    act.wait_ge(pooled_turned.sem, pooled_turned.at(b, h + 1))
                    pooled_t_ready.raised_by(nc.scalar.copy(pooled_t[:, halves[h]], high[:, halves[h]]))
                feed(b, slot, 0, 0, in_loop)
                feed(b, slot, 0, 1, in_loop)
                norm_half(b, slot, 0)
                gat(b, slot, 1, in_loop)
                gat(b, slot, 2, in_loop)
                take_xt(b, 3)
                act.wait_ge(q_psum.sem, q_psum.at(b, 1))
                q_ready.raised_by(nc.scalar.mul(queries[:, :], high, float(C) ** -0.5))
                act.wait_ge(xw_psum.sem, xw_psum.at(b, 1))
                xw_ready.raised_by(nc.scalar.copy(values[:, :, 0:C], low_t))
                for t in range(T + 2):
                    if t < T:
                        act.wait_ge(row_max.sem, row_max.at(b, t + 1))
                        if t >= 3:
                            act.wait_ge(att_turned.sem, att_turned.at(b, t - 2))
                        att_exp.raised_by(nc.scalar.activation(work[:, t % 3, :], (low, high)[t % 2], ACT.Exp,
                                                               bias=neg_max[:, t:t + 1]))
                    if t >= 2:
                        act.wait_ge(att_turned.sem, att_turned.at(b, t - 1))
                        att_t_ready.raised_by(nc.scalar.copy(probs_t[:, :, (t - 2) * P:(t - 1) * P], side_t))
                feed(b, slot, 2, 0, in_loop)
                act.wait_ge(recip_ready.sem, recip_ready.at(b, 1))
                for step in range(2):
                    src = (low_t, high_t)[step]
                    for t in range(T):
                        if step == 0 and t % 4 == 0 and exists(b, 2, B, in_loop):
                            take_turned(b + 2, slot, 2 * FEED[2][1] + t // 4)
                        if t % 4 == 0:
                            act.wait_ge(att_heads.sem, att_heads.at(b, 2 * step + t // 4 + 1))
                        att_tanh.raised_by(nc.scalar.activation(head[:, t, :], src[:, t, :], ACT.Tanh,
                                                                scale=recip[:, t:t + 1]))
                    if step == 0:
                        act.wait_ge(y_turned.sem, y_turned.at(b, 1))
                        y_ready.raised_by(nc.scalar.copy(xt[:, :], high))
                        act.wait_ge(xw_psum.sem, xw_psum.at(b, 2))
                        xw_ready.raised_by(nc.scalar.copy(values[:, :, 0:C], low_t))
                        feed(b, slot, 3, 0, in_loop)
                feed(b, slot, 3, 1, in_loop)
                norm_half(b, slot, 3)

            act.wait_ge(consts, N_CONST)
            att_tanh.raised_by(nc.scalar.copy(ident_bf[:, :], ident[:, :]))
            nc.scalar.copy(group_key[:, :], group_key_i).then_inc(setup_done, 1)
            act.wait_ge(setup_psum, 1)
            for l in range(2):
                nc.scalar.copy(gat_wt[l][:, :], side[:, l * P:(l + 1) * P])
            nc.scalar.copy(score_bias[:, 0:1], side[:, 256:257])
            nc.scalar.mul(neg_score_bias[:, 0:1], side[:, 256:257], -1.0)
            nc.scalar.mul(score_bias[:, 1:2], side[:, 256:257], 0.0)
            nc.scalar.mul(neg_score_bias[:, 1:2], side[:, 256:257], 0.0).then_inc(setup_done, 1)
            act.wait_ge(setup_psum, 2)
            for l in range(2):
                last = nc.scalar.copy(gat_srow[l][:, :, :], high[:, l * 2 * P:(l + 1) * 2 * P].rearrange(
                    "p (h c) -> p h c", h=2))
            last.then_inc(setup_done, 1)

            for b, pair in [(0, pair) for pair in range(PAIRS)] + [(1, 0), (1, 1)]:
                convert(b, b, pair)
                for t in (2 * pair, 2 * pair + 1):
                    take_turned(b, b, t)
            with act.Fori(0, LOOPED // 2) as two:
                graph(two * 2, 0, True)
                graph(two * 2 + 1, 1, True)
            for b in range(LOOPED, B):
                graph(b, b % 2, False)

        @block.tensor
        def _(pe):
            def transposes(dst, src):
                for t in range(T):
                    last = nc.tensor.transpose(dst[:, t * P:(t + 1) * P], src[:, t, :], ident[:, :])
                return last

            def turn_adj(b, slot, t):
                pe.wait_ge(adj_converted.sem, adj_converted.at(b, t + 1))
                if not (isinstance(b, int) and b == 0 and t == 0):
                    pe.wait_ge(adj_t_ready.sem, adj_t_ready.at(b, t))
                for j in range(T):
                    last = nc.tensor.transpose(turn[:, j, :], adj_bf[:, t % 2, j * P:(j + 1) * P], ident_bf[:, :])
                adj_turned.raised_by(last)

            def pack(b, slot, pair):
                if not (isinstance(b, int) and b == 0 and pair == 0):
                    pe.wait_ge(packed_read.sem, packed_read.at(b, pair))
                for t in (2 * pair, 2 * pair + 1):
                    pe.wait_ge(adj_t_ready.sem, adj_t_ready.at(b, t + 1))
                    for j in range(T):
                        last = nc.tensor.matmul(packed[:, t % 2, j * GP:(j + 1) * GP],
                                                adj_t[slot][:, j, t * P:(t + 1) * P], pack_w[:, :],
                                                start=True, stop=True)
                packed_ready.raised_by(last)

            def feed_pair(b, slot, pair):
                turn_adj(b, slot, 2 * pair)
                turn_adj(b, slot, 2 * pair + 1)
                pack(b, slot, pair)

            def feed(b, slot, layer, in_loop):
                ahead, pair = FEED[layer]
                if exists(b, ahead, B, in_loop):
                    feed_pair(b + ahead, (slot + ahead) % 2, pair)

            def project(dst, w, bias_row, tiles=range(T)):
                for t in tiles:
                    last = nc.tensor.matmul(dst[:, t, :], xt[:, t * P:(t + 1) * P], w, start=True,
                                            stop=bias_row is None)
                    if bias_row is not None:
                        last = nc.tensor.matmul(dst[:, t, :], ones[0:1, :], bias_row, start=False, stop=True)
                return last

            def turn_x(b, slot, layer):
                x_turned.raised_by(transposes(low, xs[slot]))
                pe.wait_ge(xt_ready.sem, xt_ready.at(b, layer + 1))

            def normed(b, layer):
                pe.wait_ge(x_normed.sem, x_normed.at(b, layer))
                pe.wait_ge(x_normed2.sem, x_normed2.at(b, layer))

            def gat(b, slot, layer, in_loop):
                l = layer - 1
                normed(b, layer)
                turn_x(b, slot, layer)
                for t in range(T):
                    last = nc.tensor.matmul(side[:, 2 * t:2 * t + 2], xt[:, t * P:(t + 1) * P],
                                            gat_srow[l][:, :, 0], start=True, stop=True)
                cols_psum.raised_by(last)
                w = gat_wt[0] if l == 0 else gat_w[1]
                last = nc.tensor.matmul(side[0:1, 512:512 + C], x_sum[:, 0:1], w[:, :], start=True, stop=(l == 1))
                if l == 0:
                    last = nc.tensor.matmul(side[0:1, 512:512 + C], n_nodes[:, :], b1_row[:, :], start=False,
                                            stop=True)
                sum_psum.raised_by(last)
                for half in halves:
                    last = nc.tensor.matmul(low[:, half], gat_srow[l][:, 0, :], xt[:, half], start=True, stop=True)
                row_psum.raised_by(last)
                pe.wait_ge(lanes_ready.sem, lanes_ready.at(b, layer))
                pe.wait_ge(sum_ready.sem, sum_ready.at(b, layer))
                lanes_turned.raised_by(nc.tensor.transpose(side[0:2, 512:512 + P], lane_top[:, :], ident[:, :]))
                project(high_t, w[:, :], b1_row[:, :] if l == 0 else None, range(T // 2))
                pe.wait_ge(tops_ready.sem, tops_ready.at(b, layer))
                tops_spread.raised_by(nc.tensor.matmul(side[:, 1020:1022], ones[0:2, :], both_diag[:, :],
                                                       start=True, stop=True))
                z_psum.raised_by(project(high_t, w[:, :], b1_row[:, :] if l == 0 else None, range(T // 2, T)))
                pe.wait_ge(row_gain_ready.sem, row_gain_ready.at(b, layer))
                pe.wait_ge(z_ready.sem, z_ready.at(b, layer))
                for t in range(T):
                    nc.tensor.matmul(heads[:, t, 0:C + 1], iso_row[:, t * P:(t + 1) * P], value_sum[:, :],
                                     start=(t % 2 == 0), stop=False, skip_group_check=True)
                for j in range(T):
                    pe.wait_ge(gat_probs.sem, gat_probs.at(b, l * T + j + 1))
                    for t in range(T):
                        last = nc.tensor.matmul(heads[:, t, 0:C + 1], probs_t[:, j, t * P:(t + 1) * P],
                                                values[:, j, :], start=False, stop=(j == T - 1),
                                                skip_group_check=True)
                        if j == T - 1 and t % 2 == 1:
                            gat_heads.raised_by(last)
                if layer == 1:
                    feed(b, slot, layer, in_loop)

            def graph(b, slot, in_loop):
                pe.wait_ge(x_loaded[slot].sem, x_loaded[slot].at(b, 2 - slot))
                if not (isinstance(b, int) and b == 0):
                    pe.wait_ge(att_tanh.sem, att_tanh.at(b, 0))
                x_turned.raised_by(transposes(low, xs[slot]))
                pe.wait_ge(rows_ready.sem, rows_ready.at(b, PAIRS))
                for t in range(T):
                    last = nc.tensor.transpose(side[0:1, t * P:(t + 1) * P], isolated[slot][:, t:t + 1],
                                               ident[:, :])
                iso_turned.raised_by(last)
                pe.wait_ge(xt_ready.sem, xt_ready.at(b, 1))
                for t in range(T):
                    nc.tensor.matmul(low_t[:, t, :], xt[:, t * P:(t + 1) * P], w0_sb[:, 0, :],
                                     start=(t % 4 == 0), stop=False, skip_group_check=True)
                    nc.tensor.matmul(low_t[:, t, :], ones[0:1, :], b0_row[:, :], start=False, stop=False,
                                     skip_group_check=True)
                for h in range(2):
                    tiles = range(4 * h, 4 * h + 4)
                    pe.wait_ge(rows_pooled.sem, rows_pooled.at(b, 4 * h + 4))
                    for t in tiles:
                        last = nc.tensor.transpose(high[:, t * P:(t + 1) * P], pooled[:, t, :], ident[:, :])
                    pooled_turned.raised_by(last)
                    pe.wait_ge(pooled_t_ready.sem, pooled_t_ready.at(b, h + 1))
                    for t in tiles:
                        last = nc.tensor.matmul(low_t[:, t, :], pooled_t[:, t * P:(t + 1) * P], w0_sb[:, 1, :],
                                                start=False, stop=True, skip_group_check=True)
                    sage_psum.raised_by(last)
                feed(b, slot, 0, in_loop)
                pe.wait_ge(iso_ready.sem, iso_ready.at(b, 1))
                gat(b, slot, 1, in_loop)
                gat(b, slot, 2, in_loop)
                normed(b, 3)
                turn_x(b, slot, 3)
                for half in halves:
                    last = nc.tensor.matmul(high[:, half], watt_sb[:, :], xt[:, half], start=True, stop=True)
                q_psum.raised_by(last)
                xw_psum.raised_by(project(low_t, w3_sb[0][:, :], b3_row[0][:, :]))
                pe.wait_ge(q_ready.sem, q_ready.at(b, 1))
                pe.wait_ge(xw_ready.sem, xw_ready.at(b, 1))
                for t in range(T + 2):
                    if t < T:
                        if t >= 2:
                            pe.wait_ge(att_exp.sem, att_exp.at(b, t - 1))
                        for half in halves:
                            last = nc.tensor.matmul((low, high)[t % 2][:, half], queries[:, t * P:(t + 1) * P],
                                                    xt[:, half], start=True, stop=True)
                        logits_psum.raised_by(last)
                    if t >= 2:
                        pe.wait_ge(att_masked.sem, att_masked.at(b, t - 1))
                        if t >= 3:
                            pe.wait_ge(att_t_ready.sem, att_t_ready.at(b, t - 2))
                        for m in range(T):
                            last = nc.tensor.transpose(side_t[:, m, :], work[:, (t - 2) % 3, m * P:(m + 1) * P],
                                                       ident[:, :])
                        att_turned.raised_by(last)
                pe.wait_ge(att_t_ready.sem, att_t_ready.at(b, T))
                for step in range(2):
                    for t in range(T):
                        if step == 0 and exists(b, 2, B, in_loop):
                            if t == 3:
                                turn_adj(b + 2, slot, 2 * FEED[2][1])
                            if t == 5:
                                turn_adj(b + 2, slot, 2 * FEED[2][1] + 1)
                            if t == 7:
                                pack(b + 2, slot, FEED[2][1])
                        for m in range(T):
                            last = nc.tensor.matmul((low_t, high_t)[step][:, t, :], probs_t[:, m, t * P:(t + 1) * P],
                                                    values[:, m, 0:C], start=(m == 0), stop=(m == T - 1))
                        if t % 4 == 3:
                            att_heads.raised_by(last)
                    if step == 0:
                        pe.wait_ge(att_tanh.sem, att_tanh.at(b, T))
                        y_turned.raised_by(transposes(high, head))
                        pe.wait_ge(y_ready.sem, y_ready.at(b, 1))
                        xw_psum.raised_by(project(low_t, w3_sb[1][:, :], b3_row[1][:, :]))
                        pe.wait_ge(xw_ready.sem, xw_ready.at(b, 2))
                feed(b, slot, 3, in_loop)

            pe.wait_ge(weights, WEIGHTS_IN)
            pe.wait_ge(consts, N_CONST)
            pe.wait_ge(reps_ready, 1)
            for l in range(2):
                nc.tensor.transpose(side[:, l * P:(l + 1) * P], gat_w[l][:, :], ident[:, :])
            for h in range(2):
                last = nc.tensor.matmul(side[:, 256:257], b1_rep, gat_a[0][:, h:h + 1],
                                        start=(h == 0), stop=(h == 1))
            last.then_inc(setup_psum, 1)
            pe.wait_ge(setup_done, 2)
            for l in range(2):
                w = gat_w[0] if l == 0 else gat_wt[1]
                for h in range(2):
                    last = nc.tensor.matmul(high[:, (2 * l + h) * P:(2 * l + h + 1) * P], w[:, :],
                                            gat_arep[l][:, h, :], start=True, stop=True)
            last.then_inc(setup_psum, 1)
            pe.wait_ge(setup_done, 3)

            for b, pair in [(0, pair) for pair in range(PAIRS)] + [(1, 0), (1, 1)]:
                feed_pair(b, b, pair)
            with pe.Fori(0, LOOPED // 2) as two:
                graph(two * 2, 0, True)
                graph(two * 2 + 1, 1, True)
            for b in range(LOOPED, B):
                graph(b, b % 2, False)

        @block.vector
        def _(dve):
            steps = Steps(dve)
            done, settle, link = steps.done, steps.settle, steps.link

            def bc(ap, shape):
                return ap.to_broadcast(shape)

            def top_32(dst, src):
                for k in range(0, TOP, 8):
                    if k:
                        for i in range(2):
                            done(nc.vector.match_replace(out=src[i], in_to_replace=dst[:, i, k - 8:k],
                                                         in_values=src[i], imm_value=0.0))
                        settle()
                    for i in range(2):
                        done(nc.vector.max(dst[:, i, k:k + 8], src[i]))
                    settle()

            def find_keys(b, slot, pair):
                two = slice(2 * pair, 2 * pair + 2)
                dve.wait_ge(packed_ready.sem, packed_ready.at(b, pair + 1))
                nc.vector.tensor_scalar(isolated[slot][:, two], degree[slot][:, two], 0.0, None, ALU.is_equal)
                nc.vector.tensor_scalar(connected[slot][:, two], degree[slot][:, two], 0.0, None, ALU.is_gt)
                nc.vector.tensor_scalar(pool_floor[slot][:, two], degree[slot][:, two], float(SAMPLES), LOWEST,
                                        ALU.is_gt, ALU.mult)
                for i in range(2):
                    done(nc.vector.scalar_tensor_tensor(out=keys[:, i, :], in0=packed[:, i, :], scalar=0.0,
                                                        in1=group_key[:, :], op0=ALU.is_gt, op1=ALU.mult))
                settle()
                packed_read.raised_by(nc.vector.tensor_tensor(keys[:, :, :], keys[:, :, :], packed[:, :, :], ALU.add))
                settle()
                top_32(top_keys, [keys[:, i, :] for i in range(2)])

            def find_members(b, slot, pair):
                two = slice(2 * pair, 2 * pair + 2)
                link(nc.vector.tensor_copy(top_int[:, :, :], top_keys[:, :, :]))
                done(nc.vector.tensor_scalar(top_base[:, :, :], top_int[:, :, :], GROUP, 2,
                                             ALU.logical_shift_right, ALU.logical_shift_left))
                for bit in range(GROUP):
                    done(nc.vector.tensor_scalar(top_bit[:, bit, :, :], top_int[:, :, :], bit, 1,
                                                 ALU.logical_shift_right, ALU.bitwise_and))
                settle()
                for bit in range(GROUP):
                    done(nc.vector.scalar_tensor_tensor(out=members[:, :, bit, :], in0=top_base[:, :, :],
                                                        scalar=float(bit), in1=top_bit[:, bit, :, :],
                                                        op0=ALU.subtract, op1=ALU.mult))
                settle()
                top_32(top_members, [members[:, i, :, :].rearrange("p g k -> p (g k)") for i in range(2)])
                first = top_members[:, :, 0:SAMPLES]
                link(nc.vector.scalar_tensor_tensor(out=missing[:, :, :], in0=first, scalar=0.0,
                                                    in1=bc(top_members[:, :, 0:1], [P, 2, SAMPLES]),
                                                    op0=ALU.is_equal, op1=ALU.mult))
                link(nc.vector.tensor_tensor(row_f[:, :, :], missing[:, :, :], first, ALU.add))
                link(nc.vector.tensor_scalar(row_f[:, :, :], row_f[:, :, :], -1.0, float(N), ALU.mult, ALU.add))
                rows_ready.raised_by(nc.vector.tensor_scalar(rows[:, two, :], row_f[:, :, :], float(N - 1),
                                                             row_base[:, 0:1], ALU.min, ALU.add))
                if pair == PAIRS - 1:
                    dve.wait_ge(rows_ready.sem, rows_ready.at(b, PAIRS))
                    link(nc.vector.tensor_scalar(row_base[:, :], row_base[:, :], float(N), None, ALU.add))

            def pool_tile(b, slot, t):
                ring = rows_gathered[t % RING]
                dve.wait_ge(ring.sem, ring.at(b, (t // RING + 1) * SAMPLES))
                if t == 0 and not (isinstance(b, int) and b == 0):
                    dve.wait_ge(pooled_turned.sem, pooled_turned.at(b, 0))
                link(nc.vector.tensor_reduce(
                    pooled[:, t, :], gathered[:, t % RING, :].rearrange("p (k c) -> p c k", k=SAMPLES), AX.X, ALU.max))
                rows_pooled.raised_by(nc.vector.tensor_scalar(
                    pooled[:, t, :], pooled[:, t, :], connected[slot][:, t:t + 1], pool_floor[slot][:, t:t + 1],
                    ALU.mult, ALU.max))

            def side_work(b, slot, place, in_loop):
                stages = {"keys": find_keys, "members": find_members, "pool": pool_tile}
                for stage, ahead, i in SIDE[place]:
                    if exists(b, ahead, B, in_loop):
                        stages[stage](b + ahead, (slot + ahead) % 2, i)

            def layer_norm(slot):
                for t in range(T):
                    done(nc.vector.bn_stats(stats[:, t, :], xs[slot][:, t, :]))
                settle()
                for t in range(T):
                    done(nc.vector.bn_aggr(moments[:, t, :], stats[:, t, :]))
                settle()
                link(nc.vector.tensor_scalar(spread[:, :], moments[:, :, 1], EPS, None, ALU.add))
                link(nc.vector.tensor_scalar(guess[:, :], spread[:, :].bitcast(I32), 1, None,
                                             ALU.logical_shift_right))
                link(nc.vector.tensor_scalar(rstd[:, :].bitcast(I32), guess[:, :], -1.0, RSQRT_GUESS,
                                             ALU.mult, ALU.add))
                for _ in range(3):
                    link(nc.vector.tensor_tensor(error[:, :], rstd[:, :], rstd[:, :], ALU.mult))
                    link(nc.vector.scalar_tensor_tensor(out=error[:, :], in0=error[:, :], scalar=-0.5,
                                                        in1=spread[:, :], op0=ALU.mult, op1=ALU.mult))
                    link(nc.vector.scalar_tensor_tensor(out=rstd[:, :], in0=error[:, :], scalar=1.5,
                                                        in1=rstd[:, :], op0=ALU.add, op1=ALU.mult))
                norm_scale.raised_by(nc.vector.scalar_tensor_tensor(
                    out=offset[:, :], in0=moments[:, :, 0], scalar=-1.0, in1=rstd[:, :],
                    op0=ALU.mult, op1=ALU.mult))
                for t in range(T // 2):
                    last = nc.vector.tensor_scalar(xs[slot][:, t, :], xs[slot][:, t, :], moments[:, t, 0:1],
                                                   rstd[:, t:t + 1], ALU.subtract, ALU.mult)
                x_normed.raised_by(last)

            def gat(b, slot, layer, in_loop):
                side_work(b, slot, f"gat {layer}", in_loop)
                l = layer - 1
                dve.wait_ge(cols_psum.sem, cols_psum.at(b, layer))
                cols = side[:, 0:2 * T].rearrange("p (t h) -> p h t", h=2)
                lanes_ready.raised_by(nc.vector.tensor_reduce(lane_top[:, :], cols, AX.X, ALU.max))
                dve.wait_ge(lanes_turned.sem, lanes_turned.at(b, layer))
                link(nc.vector.tensor_reduce(both_top[:, :], side[0:2, 512:512 + P], AX.X, ALU.max))
                tops_ready.raised_by(nc.vector.tensor_scalar(both_diag[:, :], ident[0:2, 0:2], both_top[:, 0:1],
                                                             None, ALU.mult))
                dve.wait_ge(tops_spread.sem, tops_spread.at(b, layer))
                link(nc.vector.tensor_scalar(neg_top[:, :], side[:, 1021:1022], -1.0, neg_score_bias[:, l:l + 1],
                                             ALU.mult, ALU.add))
                done(nc.vector.tensor_scalar(col_gap[:, :], cols[:, 1, :], score_bias[:, l:l + 1], neg_top[:, 0:1],
                                             ALU.add, ALU.add))
                link(nc.vector.tensor_scalar(crest[:, :], side[:, 1020:1021], neg_top[:, 0:1], 0.0,
                                             ALU.subtract, ALU.max))
                nc.vector.tensor_scalar(row_shift[:, :], crest[:, :], neg_top[:, 0:1], NEG_SLOPE - 1.0,
                                        ALU.add, ALU.mult)
                shifts_ready.raised_by(nc.vector.tensor_scalar(col_shift[:, :], crest[:, :], NEG_SLOPE - 1.0, None,
                                                               ALU.mult))
                dve.wait_ge(row_gain_ready.sem, row_gain_ready.at(b, layer))
                for j in range(T):
                    gat_probs.raised_by(nc.vector.scalar_tensor_tensor(
                        out=probs_t[:, j, :], in0=row_gain[:, :], scalar=col_gain[:, j:j + 1],
                        in1=adj_t[slot][:, j, :], op0=ALU.max, op1=ALU.mult))
                side_work(b, slot, f"gat {layer} heads", in_loop)
                for t in range(0, T, 2):
                    dve.wait_ge(gat_heads.sem, gat_heads.at(b, (l * T + t) // 2 + 1))
                    gat_recip.raised_by(nc.vector.reciprocal(recip[:, t:t + 2], heads[:, t:t + 2, C]))
                for h in range(2):
                    tiles = slice(4 * h, 4 * h + 4)
                    dve.wait_ge(elu_ready.sem, elu_ready.at(b, 2 * l + h + 1))
                    link(nc.vector.scalar_tensor_tensor(out=xs[slot][:, tiles, :], in0=relu_part[:, tiles, :],
                                                        scalar=-1.0, in1=xs[slot][:, tiles, :],
                                                        op0=ALU.add, op1=ALU.add))
                    link(nc.vector.scalar_tensor_tensor(out=xs[slot][:, tiles, :], in0=exp_part[:, tiles, :],
                                                        scalar=1.0, in1=xs[slot][:, tiles, :],
                                                        op0=ALU.min, op1=ALU.add))
                layer_norm(slot)

            def graph(b, slot, in_loop):
                flat = xs[slot][:, :, :].rearrange("p t c -> p (t c)")
                side_work(b, slot, "layer 0", in_loop)
                for h in range(2):
                    dve.wait_ge(sage_psum.sem, sage_psum.at(b, h + 1))
                    link(nc.vector.scalar_tensor_tensor(out=flat[:, halves[h]], in0=low[:, halves[h]], scalar=0.0,
                                                        in1=flat[:, halves[h]], op0=ALU.max, op1=ALU.add))
                layer_norm(slot)
                gat(b, slot, 1, in_loop)
                gat(b, slot, 2, in_loop)
                side_work(b, slot, "attention", in_loop)
                for t in range(T + 1):
                    if t < T:
                        dve.wait_ge(logits_psum.sem, logits_psum.at(b, t + 1))
                        row_max.raised_by(nc.vector.tensor_reduce(neg_max[:, t:t + 1], (low, high)[t % 2], AX.X,
                                                                  ALU.max, negate=True))
                    if t >= 1:
                        dve.wait_ge(att_exp.sem, att_exp.at(b, t))
                        att_masked.raised_by(nc.vector.scalar_tensor_tensor(
                            out=work[:, (t - 1) % 3, :], in0=adj_u8[slot][:, t - 1, :],
                            scalar=isolated[slot][:, t - 1:t], in1=work[:, (t - 1) % 3, :],
                            op0=ALU.add, op1=ALU.mult, accum_out=row_sum[:, t - 1:t]))
                        settle()
                dve.wait_ge(att_masked.sem, att_masked.at(b, T))
                recip_ready.raised_by(nc.vector.reciprocal(recip[:, :], row_sum[:, :]))
                side_work(b, slot, "steps", in_loop)
                dve.wait_ge(att_tanh.sem, att_tanh.at(b, 2 * T))
                link(nc.vector.tensor_tensor(flat, flat, head[:, :, :].rearrange("p t c -> p (t c)"), ALU.add))
                layer_norm(slot)
                side_work(b, slot, "end", in_loop)

            dve.wait_ge(weights, WEIGHTS_IN)
            for l in range(2):
                for h in range(2):
                    nc.vector.tensor_copy(gat_arep[l][:, h, :], bc(gat_a[l][:, h:h + 1], [P, P]))
            nc.vector.tensor_copy(b1_rep, bc(b1_col[:, 0:1], [P, P])).then_inc(reps_ready, 1)
            x_normed.raised_by(nc.vector.memset(row_base[:, :], 0.0))
            settle()
            dve.wait_ge(setup_done, 3)

            for pair in range(PAIRS):
                find_keys(0, 0, pair)
                find_members(0, 0, pair)
            for t in range(T):
                if t == 4:
                    find_keys(1, 1, 0)
                    find_members(1, 1, 0)
                pool_tile(0, 0, t)
            with dve.Fori(0, LOOPED // 2) as two:
                graph(two * 2, 0, True)
                graph(two * 2 + 1, 1, True)
            for b in range(LOOPED, B):
                graph(b, b % 2, False)


_INS = ['x', 'adj', 'L0_gnn_W', 'L0_gnn_b', 'L1_gnn_W', 'L1_gnn_b', 'L1_gnn_a', 'L2_gnn_W', 'L2_gnn_a',
        'L3_gnn_att_W', 'L3_gnn_W0', 'L3_gnn_b0', 'L3_gnn_W1', 'L3_gnn_b1']


def kernel(**inputs):
    import numpy as _np
    import concourse.bacc as _bacc
    from concourse import mybir as _mybir
    from concourse.bass_utils import run_bass_kernel_spmd as _run

    nc = _bacc.Bacc("TRN2", target_bir_lowering=False, num_devices=1)
    arrays, args = {}, []
    for name in _INS:
        a = _np.ascontiguousarray(inputs[name])
        arrays[f"in_{name}_dram"] = a
        args.append(nc.dram_tensor(f"in_{name}_dram", a.shape, _mybir.dt.from_np(a.dtype), kind="ExternalInput").ap())
    out = nc.dram_tensor("out_0_dram", inputs["x"].shape, _mybir.dt.float32, kind="ExternalOutput").ap()
    build_graph_layers(nc, *args, out)
    r = _run(nc, [arrays], core_ids=[0])
    return r.results[0]["out_0_dram"]
```

```python
import concourse.bass as bass
from concourse import mybir
from contextlib import ExitStack

F32 = mybir.dt.float32
BF16 = mybir.dt.bfloat16
F16 = mybir.dt.float16
I32 = mybir.dt.int32
U32 = mybir.dt.uint32
U8 = mybir.dt.uint8
ALU = mybir.AluOpType
ACT = mybir.ActivationFunctionType
AX = mybir.AxisListType

P = 128
SAMPLES = 25
NEG_SLOPE = 0.2
EPS = 1e-5
GROUP = 4
TOP = 32
PARTS = 3
HALF = 4
RING = 4
LOWEST = -3.0e38
CHOSEN = (2, 3)
PICK = 4
PICKS = -(-SAMPLES // PICK)
RSQRT_GUESS = float(0x5f3759df)


class Signal:

    def __init__(self, ctx, nc, name, per, unit=1, ahead=0):
        self.sem = ctx.enter_context(nc.semaphore(name))
        self.per, self.unit, self.ahead = per, unit, ahead

    def at(self, b, k):
        return b * (self.per * self.unit) + (k + self.ahead) * self.unit

    def raised_by(self, instruction):
        return instruction.then_inc(self.sem, self.unit)


class Steps:

    def __init__(self, eng):
        self.settle = eng.drain

    def done(self, instruction):
        pass

    def link(self, instruction):
        self.settle()


FEED = {0: (1, 2), 1: (1, 3), 2: (2, 0), 3: (2, 1)}
SIDE = {"layer 0": [("keys", 1, 1)],
        "gat 1": [("members", 1, 1)],
        "gat 1 heads": [("keys", 1, 2)],
        "gat 2": [("members", 1, 2)],
        "gat 2 heads": [("keys", 1, 3), ("pool", 1, 0)],
        "attention": [("members", 1, 3), ("pool", 1, 1)],
        "steps": [("pool", 1, 2), ("keys", 2, 0), ("members", 2, 0), ("pool", 1, 3), ("pool", 1, 4),
                  ("pool", 1, 5)],
        "end": [("pool", 1, 6), ("pool", 1, 7)]}


def exists(b, ahead, graphs, in_loop):
    return in_loop or b + ahead < graphs


def build_graph_layers(nc, x, adj, w0, b0, w1, b1, a1, w2, a2, watt, w3a, b3a, w3b, b3b, out):
    B, N, C = x.shape
    T = N // P
    PAIRS = T // 2
    G = N // GROUP
    GP = P // GROUP
    LOOPED = B - 2
    assert C == P and T % RING == 0 and LOOPED % 2 == 0

    x_rows = x.rearrange("b n c -> (b n) c")
    x_tiles = x.rearrange("b (t p) c -> b p t c", p=P)
    out_tiles = out.rearrange("b (t p) c -> b p t c", p=P)
    adj_tiles = adj.rearrange("b (t p) m -> b t p m", p=P)

    with ExitStack() as ctx:
        def sb(name, shape, dt=F32):
            return ctx.enter_context(nc.sbuf_tensor(name, shape, dt))

        def ps(name, shape, dt=F32):
            return ctx.enter_context(nc.psum_tensor(name, shape, dt))

        def signal(name, per, unit=1, ahead=0):
            return Signal(ctx, nc, name, per, unit, ahead)

        ident = sb("ident", [P, P])
        ident_bf = sb("ident_bf", [P, P], BF16)
        ones = sb("ones", [P, P])
        pack_w = sb("pack_w", [P, GP], BF16)
        group_key = sb("group_key", [P, G])
        w0_sb = sb("w0_sb", [P, 2, P])
        bias_in = sb("bias_in", [PARTS, 4, 1, P])
        bias_parts = sb("bias_parts", [PARTS, 4, 1, P], BF16)
        ones_bf = sb("ones_bf", [PARTS, P], BF16)
        gat_w = [sb(f"gat_w{l}", [P, P]) for l in range(2)]
        gat_wt = [sb(f"gat_wt{l}", [P, P]) for l in range(2)]
        gat_a = [sb(f"gat_a{l}", [P, 2]) for l in range(2)]
        gat_srow = [sb(f"gat_srow{l}", [P, 2, P]) for l in range(2)]
        b1_row = sb("b1_row", [1, P])
        b1_col = sb("b1_col", [P, 1])
        score_bias = sb("score_bias", [P, 2])
        neg_score_bias = sb("neg_score_bias", [P, 2])
        watt_sb = sb("watt_sb", [P, P])
        w3_sb = [sb(f"w3_sb{l}", [P, P]) for l in range(2)]

        node_id_i = sb("node_id_i", [P, T], I32)
        node_id = sb("node_id", [P, T])
        ident_h = sb("ident_h", [P, P], F16)
        list_h = sb("list_h", [P, SAMPLES], F16)

        adj_in = sb("adj_in", [P, 2, N], I32)
        adj_bf = sb("adj_bf", [P, 2, N], BF16)
        adj_u8 = [sb(f"adj_u8{i}", [P, T, N], U8) for i in range(2)]
        adj_t = [sb(f"adj_t{i}", [P, T, N], BF16) for i in range(2)]
        degree = [sb(f"degree{i}", [P, T]) for i in range(2)]
        isolated = [sb(f"isolated{i}", [P, T]) for i in range(2)]
        connected = [sb(f"connected{i}", [P, T]) for i in range(2)]
        pool_floor = [sb(f"pool_floor{i}", [P, T]) for i in range(2)]
        keys = sb("keys", [P, 2, G])
        top_keys = sb("top_keys", [P, 2, TOP])
        top_int = sb("top_int", [P, 2, TOP], I32)
        top_base = sb("top_base", [P, 2, TOP], I32)
        top_bit = sb("top_bit", [P, GROUP, 2, TOP], I32)
        members = sb("members", [P, 2, GROUP, TOP])
        top_members = sb("top_members", [P, 2, TOP])
        missing = sb("missing", [P, 2, SAMPLES])
        row_base = sb("row_base", [P, 1])
        row_f = sb("row_f", [P, 2, SAMPLES])
        rows = sb("rows", [P, T, SAMPLES], U32)
        gathered = sb("gathered", [P, RING, SAMPLES * C])
        pooled = sb("pooled", [P, T, C])
        xs = [sb(f"xs{i}", [P, T, C]) for i in range(2)]
        xt = sb("xt", [P, N])
        row_gain = sb("row_gain", [P, N])
        queries = row_gain
        work = sb("work", [P, 3, N])
        relu_part = work[:, 0, :].rearrange("p (t c) -> p t c", t=T)
        exp_part = work[:, 1, :].rearrange("p (t c) -> p t c", t=T)
        probs_t = sb("probs_t", [P, T, N])
        pooled_t = probs_t[:, 0, :]
        x_parts = [probs_t[:, i, 0:N // 2].bitcast(BF16) for i in range(PARTS)]
        x_rest = probs_t[:, 3, :]
        id_row = [probs_t[:, i, N // 2:N // 2 + PICK * P // 2].bitcast(F16) for i in range(2)]
        best_t = probs_t[:, 2, N // 2:N // 2 + P]
        pick_max = probs_t[:, 3, 0:PICKS * P].rearrange("p (g n) -> p g n", g=PICKS)
        one_hot = [[probs_t[:, 4 + 2 * i + j // 4, j % 4 * 256:j % 4 * 256 + 256].bitcast(BF16) for j in range(T)]
                   for i in range(2)]
        bias_rest = work[0:PARTS, 2, 0:4 * P].rearrange("p (b a c) -> p b a c", b=4, a=1)
        bias_part = work[0:PARTS, 2, 4 * P:6 * P].bitcast(BF16).rearrange("p (b a c) -> p b a c", b=4, a=1)
        gat_arep = [work[:, 0, l * 2 * P:(l + 1) * 2 * P].rearrange("p (h c) -> p h c", h=2) for l in range(2)]
        b1_rep = work[:, 1, 0:P]
        group_key_i = row_gain[:, 0:G].bitcast(I32)
        values = sb("values", [P, T, C + 1])
        head = xt[:, :].rearrange("p (t c) -> p t c", t=T)
        iso_row = sb("iso_row", [1, N])
        x_sum = sb("x_sum", [P, 2])
        value_sum = sb("value_sum", [1, C + 1])
        n_nodes = sb("n_nodes", [1, 1])
        top_score = sb("top_score", [P, 2])
        recip_diag = sb("recip_diag", [P, 2, P])
        neg_top = sb("neg_top", [P, 1])
        crest = sb("crest", [P, 1])
        row_shift = sb("row_shift", [P, 1])
        col_shift = sb("col_shift", [P, 1])
        col_gap = sb("col_gap", [P, T])
        col_gain = sb("col_gain", [P, T])
        recip = sb("recip", [P, T])
        neg_max = sb("neg_max", [P, T])
        row_sum = sb("row_sum", [P, T])
        stats = sb("stats", [P, T, 6])
        moments = sb("moments", [P, T, 2])
        rstd = sb("rstd", [P, T])
        spread = sb("spread", [P, T])
        guess = sb("guess", [P, T], I32)
        error = sb("error", [P, T])
        offset = sb("offset", [P, T])

        turn = ps("turn", [P, T, P], BF16)
        packed = ps("packed", [P, 2, G])
        big = ps("big", [P, 4 * 512])
        side = ps("side", [P, N])
        low, high = big[:, 0:N], big[:, N:2 * N]
        low_t = low.rearrange("p (t c) -> p t c", t=T)
        high_t = high.rearrange("p (t c) -> p t c", t=T)
        heads = big[:, :].rearrange("p (t c) -> p t c", t=T)
        side_t = side[:, :].rearrange("p (t c) -> p t c", t=T)
        halves = [slice(0, 512), slice(512, 1024)]
        id_psum = [low[:, half] for half in halves]
        picked = [high[:, half] for half in halves]

        x_split = ctx.enter_context(nc.semaphore("x_split"))
        list_ready = signal("list_ready", 1)
        ids_spread = signal("ids_spread", PICKS)
        ids_ready = signal("ids_ready", PICKS)
        one_hot_ready = signal("one_hot_ready", PICKS)
        picked_ready = signal("picked_ready", PICKS)
        pick_maxed = signal("pick_maxed", PICKS)
        best_ready = signal("best_ready", 1)
        best_turned = signal("best_turned", 1)
        weights = ctx.enter_context(nc.semaphore("weights"))
        consts = ctx.enter_context(nc.semaphore("consts"))
        reps_ready = ctx.enter_context(nc.semaphore("reps_ready"))
        setup_psum = ctx.enter_context(nc.semaphore("setup_psum"))
        setup_done = ctx.enter_context(nc.semaphore("setup_done"))
        adj_loaded = [signal(f"adj_loaded{i}", T // 2, 16) for i in range(2)]
        x_loaded = [signal(f"x_loaded{i}", 1, 8) for i in range(2)]
        out_stored = signal("out_stored", 1, 16, ahead=1)
        adj_converted = signal("adj_converted", T)
        adj_narrowed = signal("adj_narrowed", T)
        adj_turned = signal("adj_turned", T)
        adj_t_ready = signal("adj_t_ready", T)
        packed_ready = signal("packed_ready", PAIRS)
        packed_read = signal("packed_read", PAIRS)
        rows_ready = signal("rows_ready", PAIRS)
        rows_gathered = [signal(f"rows_gathered{i}", T // RING * SAMPLES, 16) for i in range(RING)]
        gathers_begun = ctx.enter_context(nc.semaphore("gathers_begun"))
        rows_pooled = signal("rows_pooled", T)
        pooled_turned = signal("pooled_turned", 2)
        pooled_t_ready = signal("pooled_t_ready", 2)
        x_turned = signal("x_turned", 8)
        xt_ready = signal("xt_ready", 8)
        sage_psum = signal("sage_psum", 2)
        iso_turned = signal("iso_turned", 1)
        iso_ready = signal("iso_ready", 1)
        norm_scale = signal("norm_scale", 4)
        x_normed = signal("x_normed", 4, ahead=1)
        x_normed2 = signal("x_normed2", 4)
        cols_psum = signal("cols_psum", 2)
        col_row_psum = signal("col_row_psum", 2)
        col_row_read = signal("col_row_read", 2)
        row_psum = signal("row_psum", 2)
        shifts_ready = signal("shifts_ready", 2)
        row_gain_ready = signal("row_gain_ready", 2)
        value_gain_ready = signal("value_gain_ready", 2)
        z_psum = signal("z_psum", 4)
        z_ready = signal("z_ready", 2)
        sum_psum = signal("sum_psum", 2)
        sum_ready = signal("sum_ready", 2)
        gat_probs = signal("gat_probs", 2 * T)
        gat_heads = signal("gat_heads", 2 * T // 2)
        gat_recip = signal("gat_recip", 2 * T // 2)
        elu_ready = signal("elu_ready", 4)
        q_psum = signal("q_psum", 1)
        q_ready = signal("q_ready", 1)
        xw_psum = signal("xw_psum", 4)
        xw_ready = signal("xw_ready", 4)
        logits_psum = signal("logits_psum", T)
        row_max = signal("row_max", T)
        att_exp = signal("att_exp", T)
        att_masked = signal("att_masked", T)
        att_turned = signal("att_turned", T)
        att_t_ready = signal("att_t_ready", T)
        diag_ready = signal("diag_ready", T)
        att_heads = signal("att_heads", 4)
        att_tanh = signal("att_tanh", 4, ahead=1)

        block = ctx.enter_context(nc.Block())
        N_CONST = 8 + GROUP
        loads = [(w0_sb[:, :, :], w0.rearrange("(h p) o -> p h o", p=P)),
                 (gat_w[0][:, :], w1), (gat_w[1][:, :], w2),
                 (gat_a[0][:, :], a1.rearrange("(h p) -> p h", p=P)),
                 (gat_a[1][:, :], a2.rearrange("(h p) a -> p (h a)", p=P)),
                 (b1_row[:, :], b1.rearrange("(a c) -> a c", a=1)),
                 (b1_col[:, :], b1.rearrange("(p a) -> p a", a=1)),
                 (watt_sb[:, :], watt), (w3_sb[0][:, :], w3a), (w3_sb[1][:, :], w3b),
                 ] + [(bias_in[:, i, :, :], bias.rearrange("(a b c) -> a b c", a=1, b=1).to_broadcast([PARTS, 1, P]))
                      for i, bias in enumerate((b0, b1, b3a, b3b))]
        WEIGHTS_IN = 16 * len(loads)

        @block.sync
        def _(sp):
            def load_adj(b, t):
                if not (isinstance(b, int) and b == 0 and t < 2):
                    sp.wait_ge(adj_narrowed.sem, adj_narrowed.at(b, t - 1))
                adj_loaded[t % 2].raised_by(sp.dma_start(adj_in[:, t % 2, :], adj_tiles[b, t]))

            def load_x(b, slot):
                if not (isinstance(b, int) and b < 2):
                    sp.wait_ge(out_stored.sem, out_stored.at(b - 1, 0))
                sp.dma_start(xs[slot][:, :, :], x_tiles[b]).then_inc(x_loaded[slot].sem, 16)

            def graph(b, slot, in_loop):
                if exists(b, 1, B, in_loop):
                    load_x(b + 1, 1 - slot)
                    for t in range(6, T):
                        load_adj(b + 1, t)
                if exists(b, 2, B, in_loop):
                    for t in range(6):
                        load_adj(b + 2, t)
                sp.wait_ge(x_normed2.sem, x_normed2.at(b, 4))
                out_stored.raised_by(sp.dma_start(out_tiles[b], xs[slot][:, :, :]))

            sp.sem_inc(out_stored.sem, out_stored.unit)
            for t in range(2):
                load_adj(0, t)
            load_x(0, 0)
            for dst, src in loads:
                with nc.allow_non_contiguous_dma(reason="small weights"):
                    sp.dma_start(dst, src).then_inc(weights, 16)
            for t in range(2, T):
                load_adj(0, t)
            for t in range(6):
                load_adj(1, t)
            with sp.Fori(0, LOOPED // 2) as two:
                graph(two * 2, 0, True)
                graph(two * 2 + 1, 1, True)
            for b in range(LOOPED, B):
                graph(b, b % 2, False)
            sp.wait_ge(out_stored.sem, out_stored.at(B, 0))

        @block.gpsimd
        def _(pool):
            nc.gpsimd.memset(ident[:, :], 0.0).then_inc(consts, 1)
            nc.gpsimd.memset(pack_w[:, :], 0.0).then_inc(consts, 1)
            nc.gpsimd.memset(ones[:, :], 1.0).then_inc(consts, 1)
            nc.gpsimd.iota(group_key_i, pattern=[[-(1 << GROUP), G]], base=G << GROUP,
                           channel_multiplier=0).then_inc(consts, 1)
            pool.wait_ge(consts, 4)
            nc.gpsimd.affine_select(out=ident[:, :], in_=ident[:, :], compare_op=ALU.not_equal, fill=1.0,
                                    base=0, pattern=[[-1, P]], channel_multiplier=1).then_inc(consts, 1)
            for bit in range(GROUP):
                nc.gpsimd.affine_select(out=pack_w[:, :], in_=pack_w[:, :], compare_op=ALU.not_equal,
                                        fill=float(1 << bit), base=bit, pattern=[[GROUP, GP]],
                                        channel_multiplier=-1).then_inc(consts, 1)
                pool.wait_ge(consts, 6 + bit)
            nc.gpsimd.memset(value_sum[:, C:C + 1], float(N)).then_inc(consts, 1)
            nc.gpsimd.memset(n_nodes[:, :], float(N)).then_inc(consts, 1)
            nc.gpsimd.iota(node_id_i[:, :], pattern=[[P, T]], base=0, channel_multiplier=1).then_inc(consts, 1)

            def gather(b, t):
                if t % 2 == 0 or isinstance(b, int):
                    pool.wait_ge(rows_ready.sem, rows_ready.at(b, t // 2 + 1))
                if not (isinstance(b, int) and b == 0 and (t < RING or t - RING in CHOSEN)):
                    pool.wait_ge(rows_pooled.sem, rows_pooled.at(b, t - RING + 1))
                pool.sem_inc(gathers_begun, 1)
                for k in range(SAMPLES):
                    rows_gathered[t % RING].raised_by(pool.indirect_dma_start(
                        out=gathered[:, t % RING, k * C:(k + 1) * C], out_offset=None, in_=x_rows,
                        in_offset=bass.IndirectOffsetOnAxis(ap=rows[:, t, k:k + 1], axis=0),
                        bounds_check=B * N - 1, oob_is_err=False))

            for t in range(T):
                if t not in CHOSEN:
                    gather(0, t)
            with pool.Fori(1, B) as b:
                for t in range(T):
                    gather(b, t)

        @block.scalar
        def _(act):
            def convert(b, slot, pair):
                for t in (2 * pair, 2 * pair + 1):
                    act.wait_ge(adj_loaded[t % 2].sem, adj_loaded[t % 2].at(b, t // 2 + 1))
                    adj_converted.raised_by(nc.scalar.activation(
                        adj_bf[:, t % 2, :], adj_in[:, t % 2, :], ACT.Copy,
                        accum_out=degree[slot][:, t:t + 1]))

            def narrow(b, slot, pair, reused=False):
                if pair == 0 and reused:
                    act.wait_ge(att_masked.sem, att_masked.at(b - 2, T))
                for t in (2 * pair, 2 * pair + 1):
                    adj_narrowed.raised_by(nc.scalar.copy(adj_u8[slot][:, t, :], adj_in[:, t % 2, :]))

            def take_turned(b, slot, t):
                act.wait_ge(adj_turned.sem, adj_turned.at(b, t + 1))
                adj_t_ready.raised_by(nc.scalar.copy(adj_t[slot][:, :, t * P:(t + 1) * P], turn[:, :, :]))

            def feed(b, slot, layer, part, in_loop):
                ahead, pair = FEED[layer]
                if exists(b, ahead, B, in_loop):
                    if part == 0:
                        convert(b + ahead, (slot + ahead) % 2, pair)
                        if layer != 2:
                            narrow(b + ahead, (slot + ahead) % 2, pair)
                    else:
                        for t in (2 * pair, 2 * pair + 1):
                            take_turned(b + ahead, (slot + ahead) % 2, t)

            def take_xt(b, layer):
                if layer == 0 and not (isinstance(b, int) and b == 0):
                    act.wait_ge(x_normed.sem, x_normed.at(b, 0))
                for h in range(2):
                    act.wait_ge(x_turned.sem, x_turned.at(b, 2 * layer + h + 1))
                    xt_ready.raised_by(nc.scalar.activation(xt[:, halves[h]], low[:, halves[h]], ACT.Copy,
                                                            accum_out=x_sum[:, h:h + 1]))

            def norm_half(b, slot, layer):
                act.wait_ge(norm_scale.sem, norm_scale.at(b, layer + 1))
                for t in range(T // 2, T):
                    if layer == 3 and t == T - 1:
                        act.wait_ge(x_normed.sem, x_normed.at(b, 4))
                    last = nc.scalar.activation(xs[slot][:, t, :], xs[slot][:, t, :], ACT.Identity,
                                                scale=rstd[:, t:t + 1], bias=offset[:, t:t + 1])
                x_normed2.raised_by(last)

            def take_xw(b, step, src):
                for h in range(2):
                    tiles = slice(HALF * h, HALF * h + HALF)
                    act.wait_ge(xw_psum.sem, xw_psum.at(b, 2 * step + h + 1))
                    xw_ready.raised_by(nc.scalar.copy(values[:, tiles, 0:C], src[:, tiles, :]))

            def gat(b, slot, layer, in_loop):
                l = layer - 1
                take_xt(b, layer)
                act.wait_ge(row_psum.sem, row_psum.at(b, layer))
                act.wait_ge(shifts_ready.sem, shifts_ready.at(b, layer))
                nc.scalar.activation(col_gain[:, :], col_gap[:, :], ACT.Exp, scale=NEG_SLOPE - 1.0,
                                     bias=col_shift[:, 0:1])
                row_gain_ready.raised_by(nc.scalar.activation(row_gain[:, :], low, ACT.Exp, scale=1.0 - NEG_SLOPE,
                                                              bias=row_shift[:, 0:1]))
                value_gain_ready.raised_by(nc.scalar.activation(
                    values[:, :, C:C + 1].rearrange("p t a -> p (t a)"), col_gap[:, :], ACT.Exp))
                act.wait_ge(sum_psum.sem, sum_psum.at(b, layer))
                sum_ready.raised_by(nc.scalar.copy(value_sum[:, 0:C], side[0:1, 512:512 + C]))
                act.wait_ge(value_gain_ready.sem, value_gain_ready.at(b, layer))
                for t in range(T):
                    if t % HALF == 0:
                        act.wait_ge(z_psum.sem, z_psum.at(b, 2 * l + t // HALF + 1))
                    last = nc.scalar.activation(values[:, t, 0:C], high_t[:, t, :], ACT.Copy,
                                                scale=values[:, t, C:C + 1])
                z_ready.raised_by(last)
                feed(b, slot, layer, 0, in_loop)
                for t in range(T):
                    if t % 2 == 0:
                        act.wait_ge(gat_recip.sem, gat_recip.at(b, (l * T + t) // 2 + 1))
                    nc.scalar.activation(relu_part[:, t, :], heads[:, t, 0:C], ACT.Relu, scale=recip[:, t:t + 1])
                    last = nc.scalar.activation(exp_part[:, t, :], heads[:, t, 0:C], ACT.Exp,
                                                scale=recip[:, t:t + 1])
                    if t % 4 == 3:
                        elu_ready.raised_by(last)
                feed(b, slot, layer, 1, in_loop)
                norm_half(b, slot, layer)

            def graph(b, slot, in_loop):
                take_xt(b, 0)
                act.wait_ge(iso_turned.sem, iso_turned.at(b, 1))
                iso_ready.raised_by(nc.scalar.copy(iso_row[:, :], side[0:1, :]))
                for h in range(2):
                    act.wait_ge(pooled_turned.sem, pooled_turned.at(b, h + 1))
                    pooled_t_ready.raised_by(nc.scalar.copy(pooled_t[:, halves[h]], high[:, halves[h]]))
                feed(b, slot, 0, 0, in_loop)
                feed(b, slot, 0, 1, in_loop)
                norm_half(b, slot, 0)
                gat(b, slot, 1, in_loop)
                gat(b, slot, 2, in_loop)
                take_xt(b, 3)
                act.wait_ge(q_psum.sem, q_psum.at(b, 1))
                q_ready.raised_by(nc.scalar.mul(queries[:, :], high, float(C) ** -0.5))
                take_xw(b, 0, low_t)
                for t in range(T + 2):
                    if t < T:
                        act.wait_ge(row_max.sem, row_max.at(b, t + 1))
                        if t >= 3:
                            act.wait_ge(att_turned.sem, att_turned.at(b, t - 2))
                        att_exp.raised_by(nc.scalar.activation(work[:, t % 3, :], (low, high)[t % 2], ACT.Exp,
                                                               bias=neg_max[:, t:t + 1]))
                    if t >= 2:
                        act.wait_ge(att_turned.sem, att_turned.at(b, t - 1))
                        att_t_ready.raised_by(nc.scalar.copy(probs_t[:, :, (t - 2) * P:(t - 1) * P], side_t))
                if exists(b, 2, B, in_loop):
                    narrow(b + 2, slot, FEED[2][1], True)
                for h in range(2):
                    act.wait_ge(att_heads.sem, att_heads.at(b, h + 1))
                    att_tanh.raised_by(nc.scalar.activation(xt[:, halves[h]], low[:, halves[h]], ACT.Tanh))
                take_xw(b, 1, high_t)
                feed(b, slot, 3, 0, in_loop)
                act.wait_ge(att_tanh.sem, att_tanh.at(b, 2))
                act.wait_ge(xw_ready.sem, xw_ready.at(b, 4))
                for h in range(2):
                    tiles = slice(HALF * h, HALF * h + HALF)
                    act.wait_ge(att_heads.sem, att_heads.at(b, 2 + h + 1))
                    att_tanh.raised_by(nc.scalar.activation(head[:, tiles, :], low_t[:, tiles, :], ACT.Tanh))
                feed(b, slot, 3, 1, in_loop)
                norm_half(b, slot, 3)

            def first_feed(b, pair):
                convert(b, b, pair)
                for t in (2 * pair, 2 * pair + 1):
                    take_turned(b, b, t)
                narrow(b, b, pair)

            act.wait_ge(consts, N_CONST)
            att_tanh.raised_by(nc.scalar.copy(ident_bf[:, :], ident[:, :]))
            nc.scalar.copy(group_key[:, :], group_key_i).then_inc(setup_done, 1)
            for pair in range(3):
                first_feed(0, pair)
            act.wait_ge(setup_psum, 1)
            for l in range(2):
                nc.scalar.copy(gat_wt[l][:, :], side[:, l * P:(l + 1) * P])
            nc.scalar.copy(score_bias[:, 0:1], side[:, 256:257])
            nc.scalar.mul(neg_score_bias[:, 0:1], side[:, 256:257], -1.0)
            nc.scalar.mul(score_bias[:, 1:2], side[:, 256:257], 0.0)
            nc.scalar.mul(neg_score_bias[:, 1:2], side[:, 256:257], 0.0).then_inc(setup_done, 1)
            act.wait_ge(setup_psum, 2)
            for l in range(2):
                last = nc.scalar.copy(gat_srow[l][:, :, :], high[:, l * 2 * P:(l + 1) * 2 * P].rearrange(
                    "p (h c) -> p h c", h=2))
            last.then_inc(setup_done, 1)

            def take_ids(i, following):
                for g in range(PICKS):
                    w = min(PICK, SAMPLES - PICK * g) * P
                    act.wait_ge(ids_spread.sem, ids_spread.at(i, g + 1))
                    if i or g >= 2:
                        act.wait_ge(one_hot_ready.sem, one_hot_ready.at(i, g - 1))
                    ids_ready.raised_by(nc.scalar.copy(id_row[(i + g) % 2][:, 0:w], id_psum[(i + g) % 2][:, 0:w]))
                    if g == PICKS // 2:
                        convert(following[0], *following)
                for t in (2 * following[1], 2 * following[1] + 1):
                    take_turned(following[0], following[0], t)
                narrow(following[0], *following)

            first_feed(0, 3)
            take_ids(0, (1, 0))
            take_ids(1, (1, 1))
            with act.Fori(0, LOOPED // 2) as two:
                graph(two * 2, 0, True)
                graph(two * 2 + 1, 1, True)
            for b in range(LOOPED, B):
                graph(b, b % 2, False)

        @block.tensor
        def _(pe):
            def turn_adj(b, slot, t):
                pe.wait_ge(adj_converted.sem, adj_converted.at(b, t + 1))
                if not (isinstance(b, int) and b == 0 and t == 0):
                    pe.wait_ge(adj_t_ready.sem, adj_t_ready.at(b, t))
                for j in range(T):
                    last = nc.tensor.transpose(turn[:, j, :], adj_bf[:, t % 2, j * P:(j + 1) * P], ident_bf[:, :])
                adj_turned.raised_by(last)

            def pack(b, slot, pair):
                if not (isinstance(b, int) and b == 0 and pair == 0):
                    pe.wait_ge(packed_read.sem, packed_read.at(b, pair))
                for t in (2 * pair, 2 * pair + 1):
                    pe.wait_ge(adj_t_ready.sem, adj_t_ready.at(b, t + 1))
                    for j in range(T):
                        last = nc.tensor.matmul(packed[:, t % 2, j * GP:(j + 1) * GP],
                                                adj_t[slot][:, j, t * P:(t + 1) * P], pack_w[:, :],
                                                start=True, stop=True)
                packed_ready.raised_by(last)

            def feed_pair(b, slot, pair):
                turn_adj(b, slot, 2 * pair)
                turn_adj(b, slot, 2 * pair + 1)
                pack(b, slot, pair)

            def feed(b, slot, layer, in_loop):
                ahead, pair = FEED[layer]
                if exists(b, ahead, B, in_loop):
                    feed_pair(b + ahead, (slot + ahead) % 2, pair)

            def add_bias(dst, i):
                for h in range(2):
                    nc.tensor.matmul(dst[:, HALF * h:HALF * h + HALF, :], ones_bf[:, :],
                                     bias_parts[:, i, :, :].to_broadcast([PARTS, HALF, P]),
                                     start=True, stop=False, skip_group_check=True)

            def project(dst, w, tiles, biased):
                for t in tiles:
                    last = nc.tensor.matmul(dst[:, t, :], xt[:, t * P:(t + 1) * P], w, start=not biased,
                                            stop=True, skip_group_check=True)
                return last

            def turn_x(b, slot, layer):
                for h in range(2):
                    if layer:
                        half_normed = (x_normed, x_normed2)[h]
                        pe.wait_ge(half_normed.sem, half_normed.at(b, layer))
                    for t in range(HALF * h, HALF * h + HALF):
                        last = nc.tensor.transpose(low[:, t * P:(t + 1) * P], xs[slot][:, t, :], ident[:, :])
                    x_turned.raised_by(last)

            def gat(b, slot, layer, in_loop):
                l = layer - 1
                w = gat_wt[0] if l == 0 else gat_w[1]
                turn_x(b, slot, layer)
                for h in range(2):
                    pe.wait_ge(xt_ready.sem, xt_ready.at(b, 2 * layer + h + 1))
                    last = nc.tensor.matmul(high[:, halves[h]], gat_srow[l][:, 1, :], xt[:, halves[h]],
                                            start=True, stop=True)
                col_row_psum.raised_by(last)
                for half in halves:
                    last = nc.tensor.matmul(low[:, half], gat_srow[l][:, 0, :], xt[:, half], start=True, stop=True)
                row_psum.raised_by(last)
                for t in range(T):
                    last = nc.tensor.matmul(side[:, 2 * t:2 * t + 2], xt[:, t * P:(t + 1) * P],
                                            gat_srow[l][:, :, 0], start=True, stop=True)
                cols_psum.raised_by(last)
                for h in range(2):
                    last = nc.tensor.matmul(side[0:1, 512:512 + C], x_sum[:, h:h + 1], w[:, :], start=(h == 0),
                                            stop=(l == 1 and h == 1))
                if l == 0:
                    last = nc.tensor.matmul(side[0:1, 512:512 + C], n_nodes[:, :], b1_row[:, :], start=False,
                                            stop=True)
                sum_psum.raised_by(last)
                pe.wait_ge(col_row_read.sem, col_row_read.at(b, layer))
                if l == 0:
                    add_bias(high_t, 1)
                z_psum.raised_by(project(high_t, w[:, :], range(HALF), l == 0))
                z_psum.raised_by(project(high_t, w[:, :], range(HALF, T), l == 0))
                pe.wait_ge(row_gain_ready.sem, row_gain_ready.at(b, layer))
                pe.wait_ge(sum_ready.sem, sum_ready.at(b, layer))
                for t in range(T):
                    if t == HALF:
                        pe.wait_ge(z_ready.sem, z_ready.at(b, layer))
                    nc.tensor.matmul(heads[:, t, 0:C + 1], iso_row[:, t * P:(t + 1) * P], value_sum[:, :],
                                     start=(t % 2 == 0), stop=False, skip_group_check=True)
                for j in range(T):
                    pe.wait_ge(gat_probs.sem, gat_probs.at(b, l * T + j + 1))
                    for t in range(T):
                        last = nc.tensor.matmul(heads[:, t, 0:C + 1], probs_t[:, j, t * P:(t + 1) * P],
                                                values[:, j, :], start=False, stop=(j == T - 1),
                                                skip_group_check=True)
                        if j == T - 1 and t % 2 == 1:
                            gat_heads.raised_by(last)
                feed(b, slot, layer, in_loop)

            def graph(b, slot, in_loop):
                pe.wait_ge(x_loaded[slot].sem, x_loaded[slot].at(b, 2 - slot))
                if not (isinstance(b, int) and b == 0):
                    pe.wait_ge(att_tanh.sem, att_tanh.at(b, 0))
                turn_x(b, slot, 0)
                pe.wait_ge(rows_ready.sem, rows_ready.at(b, PAIRS))
                for t in range(T):
                    last = nc.tensor.transpose(side[0:1, t * P:(t + 1) * P], isolated[slot][:, t:t + 1],
                                               ident[:, :])
                iso_turned.raised_by(last)
                pe.wait_ge(xt_ready.sem, xt_ready.at(b, 2))
                add_bias(low_t, 0)
                project(low_t, w0_sb[:, 0, :], range(T), True)
                for h in range(2):
                    tiles = range(4 * h, 4 * h + 4)
                    pe.wait_ge(rows_pooled.sem, rows_pooled.at(b, 4 * h + 4))
                    for t in tiles:
                        last = nc.tensor.transpose(high[:, t * P:(t + 1) * P], pooled[:, t, :], ident[:, :])
                    pooled_turned.raised_by(last)
                    pe.wait_ge(pooled_t_ready.sem, pooled_t_ready.at(b, h + 1))
                    for t in tiles:
                        last = nc.tensor.matmul(low_t[:, t, :], pooled_t[:, t * P:(t + 1) * P], w0_sb[:, 1, :],
                                                start=False, stop=True, skip_group_check=True)
                    sage_psum.raised_by(last)
                feed(b, slot, 0, in_loop)
                pe.wait_ge(iso_ready.sem, iso_ready.at(b, 1))
                gat(b, slot, 1, in_loop)
                gat(b, slot, 2, in_loop)
                turn_x(b, slot, 3)
                for h in range(2):
                    pe.wait_ge(xt_ready.sem, xt_ready.at(b, 6 + h + 1))
                    last = nc.tensor.matmul(high[:, halves[h]], watt_sb[:, :], xt[:, halves[h]], start=True,
                                            stop=True)
                q_psum.raised_by(last)
                add_bias(low_t, 2)
                for h in range(2):
                    xw_psum.raised_by(project(low_t, w3_sb[0][:, :], range(HALF * h, HALF * h + HALF), True))
                pe.wait_ge(q_ready.sem, q_ready.at(b, 1))
                pe.wait_ge(xw_ready.sem, xw_ready.at(b, 2))
                for t in range(T + 2):
                    if t < T:
                        if t >= 2:
                            pe.wait_ge(att_exp.sem, att_exp.at(b, t - 1))
                        for half in halves:
                            last = nc.tensor.matmul((low, high)[t % 2][:, half], queries[:, t * P:(t + 1) * P],
                                                    xt[:, half], start=True, stop=True)
                        logits_psum.raised_by(last)
                    if t >= 2:
                        pe.wait_ge(diag_ready.sem, diag_ready.at(b, t - 1))
                        if t >= 3:
                            pe.wait_ge(att_t_ready.sem, att_t_ready.at(b, t - 2))
                        for m in range(T):
                            last = nc.tensor.matmul(side_t[:, m, :], work[:, (t - 2) % 3, m * P:(m + 1) * P],
                                                    recip_diag[:, t % 2, :], start=True, stop=True)
                        att_turned.raised_by(last)
                pe.wait_ge(att_t_ready.sem, att_t_ready.at(b, T))
                for h in range(2):
                    for m in range(T):
                        last = nc.tensor.matmul(low[:, halves[h]], values[:, m, 0:C], probs_t[:, m, halves[h]],
                                                start=(m == 0), stop=(m == T - 1))
                    att_heads.raised_by(last)
                add_bias(high_t, 3)
                for h in range(2):
                    pe.wait_ge(att_tanh.sem, att_tanh.at(b, h + 1))
                    xw_psum.raised_by(project(high_t, w3_sb[1][:, :], range(HALF * h, HALF * h + HALF), True))
                pe.wait_ge(xw_ready.sem, xw_ready.at(b, 4))
                for t in range(T):
                    for m in range(T):
                        last = nc.tensor.matmul(low_t[:, t, :], probs_t[:, m, t * P:(t + 1) * P], values[:, m, 0:C],
                                                start=(m == 0), stop=(m == T - 1))
                    if t % HALF == HALF - 1:
                        att_heads.raised_by(last)
                feed(b, slot, 3, in_loop)

            pe.wait_ge(consts, N_CONST)
            pe.wait_ge(setup_done, 1)
            for pair in range(3):
                feed_pair(0, 0, pair)
            pe.wait_ge(weights, WEIGHTS_IN)
            pe.wait_ge(reps_ready, 1)
            for l in range(2):
                nc.tensor.transpose(side[:, l * P:(l + 1) * P], gat_w[l][:, :], ident[:, :])
            for h in range(2):
                last = nc.tensor.matmul(side[:, 256:257], b1_rep, gat_a[0][:, h:h + 1],
                                        start=(h == 0), stop=(h == 1))
            last.then_inc(setup_psum, 1)
            pe.wait_ge(setup_done, 2)
            for l in range(2):
                w = gat_w[0] if l == 0 else gat_wt[1]
                for h in range(2):
                    last = nc.tensor.matmul(high[:, (2 * l + h) * P:(2 * l + h + 1) * P], w[:, :],
                                            gat_arep[l][:, h, :], start=True, stop=True)
            last.then_inc(setup_psum, 1)
            pe.wait_ge(setup_done, 3)

            def pick_rows(i):
                def spread_ids(g):
                    if i or g >= 2:
                        pe.wait_ge(ids_ready.sem, ids_ready.at(i, g - 1))
                    for k in range(PICK * g, min(PICK * g + PICK, SAMPLES)):
                        last = nc.tensor.matmul(id_psum[(i + g) % 2][:, k % PICK * P:(k % PICK + 1) * P],
                                                list_h[:, k:k + 1].to_broadcast([P, P]), ident_h[:, :],
                                                start=True, stop=True)
                    ids_spread.raised_by(last)

                pe.wait_ge(list_ready.sem, list_ready.at(i, 1))
                spread_ids(0)
                spread_ids(1)
                for g in range(PICKS):
                    w = min(PICK, SAMPLES - PICK * g) * P
                    pe.wait_ge(one_hot_ready.sem, one_hot_ready.at(i, g + 1))
                    if i or g >= 2:
                        pe.wait_ge(pick_maxed.sem, pick_maxed.at(i, g - 1))
                    for j in range(T):
                        for part in range(PARTS):
                            last = nc.tensor.matmul(picked[(i + g) % 2][:, 0:w], x_parts[part][:, j * P:(j + 1) * P],
                                                    one_hot[(i + g) % 2][j][:, 0:w],
                                                    start=(j == 0 and part == 0),
                                                    stop=(j == T - 1 and part == PARTS - 1))
                    picked_ready.raised_by(last)
                    if g + 2 < PICKS:
                        spread_ids(g + 2)
                pe.wait_ge(best_ready.sem, best_ready.at(i, 1))
                best_turned.raised_by(nc.tensor.transpose(side[:, 0:P], best_t, ident[:, :]))

            feed_pair(0, 0, 3)
            pe.wait_ge(x_split, 1)
            for i in range(len(CHOSEN)):
                pick_rows(i)
                feed_pair(1, 1, i)
            pe.wait_ge(rows_pooled.sem, rows_pooled.at(0, CHOSEN[-1] + 1))
            with pe.Fori(0, LOOPED // 2) as two:
                graph(two * 2, 0, True)
                graph(two * 2 + 1, 1, True)
            for b in range(LOOPED, B):
                graph(b, b % 2, False)

        @block.vector
        def _(dve):
            steps = Steps(dve)
            done, settle, link = steps.done, steps.settle, steps.link

            def bc(ap, shape):
                return ap.to_broadcast(shape)

            def top_32(dst, src):
                for k in range(0, TOP, 8):
                    if k:
                        for i in range(2):
                            done(nc.vector.match_replace(out=src[i], in_to_replace=dst[:, i, k - 8:k],
                                                         in_values=src[i], imm_value=0.0))
                        settle()
                    for i in range(2):
                        done(nc.vector.max(dst[:, i, k:k + 8], src[i]))
                    settle()

            def find_keys(b, slot, pair):
                two = slice(2 * pair, 2 * pair + 2)
                dve.wait_ge(packed_ready.sem, packed_ready.at(b, pair + 1))
                nc.vector.tensor_scalar(isolated[slot][:, two], degree[slot][:, two], 0.0, None, ALU.is_equal)
                nc.vector.tensor_scalar(connected[slot][:, two], degree[slot][:, two], 0.0, None, ALU.is_gt)
                nc.vector.tensor_scalar(pool_floor[slot][:, two], degree[slot][:, two], float(SAMPLES), LOWEST,
                                        ALU.is_gt, ALU.mult)
                for i in range(2):
                    done(nc.vector.scalar_tensor_tensor(out=keys[:, i, :], in0=packed[:, i, :], scalar=0.0,
                                                        in1=group_key[:, :], op0=ALU.is_gt, op1=ALU.mult))
                settle()
                packed_read.raised_by(nc.vector.tensor_tensor(keys[:, :, :], keys[:, :, :], packed[:, :, :], ALU.add))
                settle()
                top_32(top_keys, [keys[:, i, :] for i in range(2)])

            def find_members(b, slot, pair):
                two = slice(2 * pair, 2 * pair + 2)
                link(nc.vector.tensor_copy(top_int[:, :, :], top_keys[:, :, :]))
                done(nc.vector.tensor_scalar(top_base[:, :, :], top_int[:, :, :], GROUP, 2,
                                             ALU.logical_shift_right, ALU.logical_shift_left))
                for bit in range(GROUP):
                    done(nc.vector.tensor_scalar(top_bit[:, bit, :, :], top_int[:, :, :], bit, 1,
                                                 ALU.logical_shift_right, ALU.bitwise_and))
                settle()
                for bit in range(GROUP):
                    done(nc.vector.scalar_tensor_tensor(out=members[:, :, bit, :], in0=top_base[:, :, :],
                                                        scalar=float(bit), in1=top_bit[:, bit, :, :],
                                                        op0=ALU.subtract, op1=ALU.mult))
                settle()
                top_32(top_members, [members[:, i, :, :].rearrange("p g k -> p (g k)") for i in range(2)])
                first = top_members[:, :, 0:SAMPLES]
                link(nc.vector.scalar_tensor_tensor(out=missing[:, :, :], in0=first, scalar=0.0,
                                                    in1=bc(top_members[:, :, 0:1], [P, 2, SAMPLES]),
                                                    op0=ALU.is_equal, op1=ALU.mult))
                link(nc.vector.tensor_tensor(row_f[:, :, :], missing[:, :, :], first, ALU.add))
                link(nc.vector.tensor_scalar(row_f[:, :, :], row_f[:, :, :], -1.0, float(N), ALU.mult, ALU.add))
                rows_ready.raised_by(nc.vector.tensor_scalar(rows[:, two, :], row_f[:, :, :], float(N - 1),
                                                             row_base[:, 0:1], ALU.min, ALU.add))
                if pair == PAIRS - 1:
                    dve.wait_ge(rows_ready.sem, rows_ready.at(b, PAIRS))
                    link(nc.vector.tensor_scalar(row_base[:, :], row_base[:, :], float(N), None, ALU.add))

            def pool_tile(b, slot, t):
                ring = rows_gathered[t % RING]
                skipped = sum(c % RING == t % RING and not (isinstance(b, int) and b == 0 and c > t)
                              for c in CHOSEN)
                dve.wait_ge(ring.sem, ring.at(b, (t // RING + 1 - skipped) * SAMPLES))
                if t == 0 and not (isinstance(b, int) and b == 0):
                    dve.wait_ge(pooled_turned.sem, pooled_turned.at(b, 0))
                link(nc.vector.tensor_reduce(
                    pooled[:, t, :], gathered[:, t % RING, :].rearrange("p (k c) -> p c k", k=SAMPLES), AX.X, ALU.max))
                rows_pooled.raised_by(nc.vector.tensor_scalar(
                    pooled[:, t, :], pooled[:, t, :], connected[slot][:, t:t + 1], pool_floor[slot][:, t:t + 1],
                    ALU.mult, ALU.max))

            def side_work(b, slot, place, in_loop):
                stages = {"keys": find_keys, "members": find_members, "pool": pool_tile}
                for stage, ahead, i in SIDE[place]:
                    if exists(b, ahead, B, in_loop):
                        stages[stage](b + ahead, (slot + ahead) % 2, i)

            def layer_norm(slot):
                for t in range(T):
                    done(nc.vector.bn_stats(stats[:, t, :], xs[slot][:, t, :]))
                settle()
                for t in range(T):
                    done(nc.vector.bn_aggr(moments[:, t, :], stats[:, t, :]))
                settle()
                link(nc.vector.tensor_scalar(spread[:, :], moments[:, :, 1], EPS, None, ALU.add))
                link(nc.vector.tensor_scalar(guess[:, :], spread[:, :].bitcast(I32), 1, None,
                                             ALU.logical_shift_right))
                link(nc.vector.tensor_scalar(rstd[:, :].bitcast(I32), guess[:, :], -1.0, RSQRT_GUESS,
                                             ALU.mult, ALU.add))
                for _ in range(3):
                    link(nc.vector.tensor_tensor(error[:, :], rstd[:, :], rstd[:, :], ALU.mult))
                    link(nc.vector.scalar_tensor_tensor(out=error[:, :], in0=error[:, :], scalar=-0.5,
                                                        in1=spread[:, :], op0=ALU.mult, op1=ALU.mult))
                    link(nc.vector.scalar_tensor_tensor(out=rstd[:, :], in0=error[:, :], scalar=1.5,
                                                        in1=rstd[:, :], op0=ALU.add, op1=ALU.mult))
                norm_scale.raised_by(nc.vector.scalar_tensor_tensor(
                    out=offset[:, :], in0=moments[:, :, 0], scalar=-1.0, in1=rstd[:, :],
                    op0=ALU.mult, op1=ALU.mult))
                for t in range(T // 2):
                    last = nc.vector.tensor_scalar(xs[slot][:, t, :], xs[slot][:, t, :], moments[:, t, 0:1],
                                                   rstd[:, t:t + 1], ALU.subtract, ALU.mult)
                x_normed.raised_by(last)

            def gat(b, slot, layer, in_loop):
                side_work(b, slot, f"gat {layer}", in_loop)
                l = layer - 1
                dve.wait_ge(col_row_psum.sem, col_row_psum.at(b, layer))
                col_row_read.raised_by(nc.vector.tensor_reduce(top_score[:, 1:2], high, AX.X, ALU.max))
                dve.wait_ge(row_psum.sem, row_psum.at(b, layer))
                link(nc.vector.tensor_reduce(top_score[:, 0:1], low, AX.X, ALU.max))
                link(nc.vector.tensor_scalar(neg_top[:, :], top_score[:, 1:2], -1.0, neg_score_bias[:, l:l + 1],
                                             ALU.mult, ALU.add))
                dve.wait_ge(cols_psum.sem, cols_psum.at(b, layer))
                cols = side[:, 0:2 * T].rearrange("p (t h) -> p h t", h=2)
                done(nc.vector.tensor_scalar(col_gap[:, :], cols[:, 1, :], score_bias[:, l:l + 1], neg_top[:, 0:1],
                                             ALU.add, ALU.add))
                link(nc.vector.tensor_scalar(crest[:, :], top_score[:, 0:1], neg_top[:, 0:1], 0.0,
                                             ALU.subtract, ALU.max))
                nc.vector.tensor_scalar(row_shift[:, :], crest[:, :], neg_top[:, 0:1], NEG_SLOPE - 1.0,
                                        ALU.add, ALU.mult)
                shifts_ready.raised_by(nc.vector.tensor_scalar(col_shift[:, :], crest[:, :], NEG_SLOPE - 1.0, None,
                                                               ALU.mult))
                dve.wait_ge(row_gain_ready.sem, row_gain_ready.at(b, layer))
                for j in range(T):
                    gat_probs.raised_by(nc.vector.scalar_tensor_tensor(
                        out=probs_t[:, j, :], in0=row_gain[:, :], scalar=col_gain[:, j:j + 1],
                        in1=adj_t[slot][:, j, :], op0=ALU.max, op1=ALU.mult))
                side_work(b, slot, f"gat {layer} heads", in_loop)
                for t in range(0, T, 2):
                    dve.wait_ge(gat_heads.sem, gat_heads.at(b, (l * T + t) // 2 + 1))
                    gat_recip.raised_by(nc.vector.reciprocal(recip[:, t:t + 2], heads[:, t:t + 2, C]))
                for h in range(2):
                    tiles = slice(4 * h, 4 * h + 4)
                    dve.wait_ge(elu_ready.sem, elu_ready.at(b, 2 * l + h + 1))
                    link(nc.vector.scalar_tensor_tensor(out=xs[slot][:, tiles, :], in0=relu_part[:, tiles, :],
                                                        scalar=-1.0, in1=xs[slot][:, tiles, :],
                                                        op0=ALU.add, op1=ALU.add))
                    link(nc.vector.scalar_tensor_tensor(out=xs[slot][:, tiles, :], in0=exp_part[:, tiles, :],
                                                        scalar=1.0, in1=xs[slot][:, tiles, :],
                                                        op0=ALU.min, op1=ALU.add))
                layer_norm(slot)

            def graph(b, slot, in_loop):
                flat = xs[slot][:, :, :].rearrange("p t c -> p (t c)")
                side_work(b, slot, "layer 0", in_loop)
                for h in range(2):
                    dve.wait_ge(sage_psum.sem, sage_psum.at(b, h + 1))
                    link(nc.vector.scalar_tensor_tensor(out=flat[:, halves[h]], in0=low[:, halves[h]], scalar=0.0,
                                                        in1=flat[:, halves[h]], op0=ALU.max, op1=ALU.add))
                layer_norm(slot)
                gat(b, slot, 1, in_loop)
                gat(b, slot, 2, in_loop)
                side_work(b, slot, "attention", in_loop)
                for t in range(T + 1):
                    if t < T:
                        dve.wait_ge(logits_psum.sem, logits_psum.at(b, t + 1))
                        row_max.raised_by(nc.vector.tensor_reduce(neg_max[:, t:t + 1], (low, high)[t % 2], AX.X,
                                                                  ALU.max, negate=True))
                    if t >= 1:
                        dve.wait_ge(att_exp.sem, att_exp.at(b, t))
                        att_masked.raised_by(nc.vector.scalar_tensor_tensor(
                            out=work[:, (t - 1) % 3, :], in0=adj_u8[slot][:, t - 1, :],
                            scalar=isolated[slot][:, t - 1:t], in1=work[:, (t - 1) % 3, :],
                            op0=ALU.add, op1=ALU.mult, accum_out=row_sum[:, t - 1:t]))
                        settle()
                        link(nc.vector.reciprocal(recip[:, t - 1:t], row_sum[:, t - 1:t]))
                        if t >= 3:
                            dve.wait_ge(att_turned.sem, att_turned.at(b, t - 2))
                        diag_ready.raised_by(nc.vector.tensor_scalar(
                            recip_diag[:, (t + 1) % 2, :], ident[:, :], recip[:, t - 1:t], None, ALU.mult))
                side_work(b, slot, "steps", in_loop)
                for h in range(2):
                    dve.wait_ge(att_tanh.sem, att_tanh.at(b, 2 + h + 1))
                    link(nc.vector.tensor_tensor(
                        flat[:, halves[h]], flat[:, halves[h]],
                        head[:, HALF * h:HALF * h + HALF, :].rearrange("p t c -> p (t c)"), ALU.add))
                layer_norm(slot)
                side_work(b, slot, "end", in_loop)

            x_normed.raised_by(nc.vector.memset(row_base[:, :], 0.0))
            dve.wait_ge(consts, N_CONST)
            settle()
            dve.wait_ge(setup_done, 1)
            for pair in range(2):
                find_keys(0, 0, pair)
                find_members(0, 0, pair)

            dve.wait_ge(weights, WEIGHTS_IN)
            for l in range(2):
                for h in range(2):
                    nc.vector.tensor_copy(gat_arep[l][:, h, :], bc(gat_a[l][:, h:h + 1], [P, P]))
            nc.vector.tensor_copy(b1_rep, bc(b1_col[:, 0:1], [P, P])).then_inc(reps_ready, 1)
            nc.vector.memset(ones_bf[:, :], 1.0)
            for k in range(PARTS):
                link(nc.vector.tensor_copy(bias_part, bias_in[:, :, :, :] if k == 0 else bias_rest))
                link(nc.vector.tensor_tensor(bias_rest, bias_in[:, :, :, :] if k == 0 else bias_rest, bias_part,
                                             ALU.subtract))
                if k == 0:
                    last = nc.vector.tensor_scalar(bias_parts[:, :, :, :], bias_part, ident[0:PARTS, 0:1], None,
                                                   ALU.mult)
                else:
                    last = nc.vector.scalar_tensor_tensor(
                        out=bias_parts[:, :, :, :], in0=bias_part, scalar=ident[0:PARTS, k:k + 1],
                        in1=bias_parts[:, :, :, :], op0=ALU.mult, op1=ALU.add)
                settle()
            def make_one_hot(i, g):
                w = min(PICK, SAMPLES - PICK * g) * P
                dve.wait_ge(ids_ready.sem, ids_ready.at(i, g + 1))
                if i or g >= 2:
                    dve.wait_ge(picked_ready.sem, picked_ready.at(i, g - 1))
                for j in range(T):
                    last = nc.vector.tensor_scalar(one_hot[(i + g) % 2][j][:, 0:w], id_row[(i + g) % 2][:, 0:w],
                                                   node_id[:, j:j + 1], None, ALU.is_equal)
                one_hot_ready.raised_by(last)

            def max_pick(i, g):
                n = min(PICK, SAMPLES - PICK * g)
                dve.wait_ge(picked_ready.sem, picked_ready.at(i, g + 1))
                pick_maxed.raised_by(nc.vector.tensor_reduce(
                    pick_max[:, g, :], picked[(i + g) % 2][:, 0:n * P].rearrange("p (k n) -> p n k", k=n),
                    AX.X, ALU.max))

            def pool_chosen(i, meanwhile):
                t = CHOSEN[i]
                if i:
                    dve.wait_ge(ids_spread.sem, ids_spread.at(i, 0))
                list_ready.raised_by(nc.vector.tensor_copy(list_h[:, :], rows[:, t, :]))
                for g in range(PICKS):
                    make_one_hot(i, g)
                    if g >= 1:
                        max_pick(i, g - 1)
                    for stage, b, k in meanwhile.get(g, []):
                        stage(b, b, k)
                max_pick(i, PICKS - 1)
                settle()
                best_ready.raised_by(nc.vector.tensor_reduce(
                    best_t, pick_max[:, :, :].rearrange("p g n -> p n g"), AX.X, ALU.max))
                dve.wait_ge(best_turned.sem, best_turned.at(i, 1))
                rows_pooled.raised_by(nc.vector.tensor_scalar(
                    pooled[:, t, :], side[:, 0:P], connected[0][:, t:t + 1], pool_floor[0][:, t:t + 1],
                    ALU.mult, ALU.max))

            find_keys(0, 0, 2)
            find_members(0, 0, 2)
            nc.vector.tensor_copy(node_id[:, :], node_id_i[:, :])
            nc.vector.tensor_copy(ident_h[:, :], ident[:, :])
            dve.wait_ge(x_loaded[0].sem, x_loaded[0].at(0, 2))
            x_flat = xs[0][:, :, :].rearrange("p t c -> p (t c)")
            for part in range(PARTS):
                rest = x_rest if part else x_flat
                link(nc.vector.tensor_copy(x_parts[part], rest))
                if part < PARTS - 1:
                    link(nc.vector.tensor_tensor(x_rest, rest, x_parts[part], ALU.subtract))
            dve.sem_inc(x_split, 1)
            pool_tile(0, 0, 0)
            pool_chosen(0, {3: [(pool_tile, 0, 1)], 5: [(find_keys, 0, 3)]})
            pool_chosen(1, {0: [(find_members, 0, 3)], 2: [(find_keys, 1, 0)], 4: [(find_members, 1, 0)]})
            for t in range(4, T):
                pool_tile(0, 0, t)
            dve.wait_ge(setup_done, 3)
            with dve.Fori(0, LOOPED // 2) as two:
                graph(two * 2, 0, True)
                graph(two * 2 + 1, 1, True)
            for b in range(LOOPED, B):
                graph(b, b % 2, False)


_INS = ['x', 'adj', 'L0_gnn_W', 'L0_gnn_b', 'L1_gnn_W', 'L1_gnn_b', 'L1_gnn_a', 'L2_gnn_W', 'L2_gnn_a',
        'L3_gnn_att_W', 'L3_gnn_W0', 'L3_gnn_b0', 'L3_gnn_W1', 'L3_gnn_b1']


def kernel(**inputs):
    import numpy as _np
    import concourse.bacc as _bacc
    from concourse import mybir as _mybir
    from concourse.bass_utils import run_bass_kernel_spmd as _run

    nc = _bacc.Bacc("TRN2", target_bir_lowering=False, num_devices=1)
    arrays, args = {}, []
    for name in _INS:
        a = _np.ascontiguousarray(inputs[name])
        arrays[f"in_{name}_dram"] = a
        args.append(nc.dram_tensor(f"in_{name}_dram", a.shape, _mybir.dt.from_np(a.dtype), kind="ExternalInput").ap())
    out = nc.dram_tensor("out_0_dram", inputs["x"].shape, _mybir.dt.float32, kind="ExternalOutput").ap()
    build_graph_layers(nc, *args, out)
    r = _run(nc, [arrays], core_ids=[0])
    return r.results[0]["out_0_dram"]
```
